# Optimizing a Trainium2 kernel written in Bass

```python
import numpy as np
import jax
import jax.numpy as jnp

def _softmax(x, axis=-1):
    return jax.nn.softmax(x, axis=axis)

def _gelu(x):
    return jax.nn.gelu(x, approximate=True)

def _silu(x):
    return jax.nn.silu(x)

def _sigmoid(x):
    return jax.nn.sigmoid(x)

def _layernorm(x, axis=-1, eps=1e-05):
    m = jnp.mean(x, axis=axis, keepdims=True)
    v = jnp.var(x, axis=axis, keepdims=True)
    return (x - m) / jnp.sqrt(v + eps)

def _scatter_add(tgt, idx, src, axis=0):
    return tgt.at[idx].add(src)

def _segment_sum(src, seg, n):
    return jax.ops.segment_sum(src, seg, n)
kernel_name = 'mk_gnn_ffn_d1_gnn_r8_36d904'

def setup_inputs(seed: int=0):
    np.random.seed(seed)
    _w = jnp.asarray

    def _rec_inputs():
        import jax
        import jax.numpy as jnp
        _gk = jax.random.key(seed)
        x = -0.0002117 + 1 * jax.random.normal(jax.random.fold_in(_gk, 1), (1250, 512), jnp.float32)
        src = jax.random.randint(jax.random.fold_in(_gk, 2), (40000,), 0, 1250, jnp.int32)
        dst = jax.random.randint(jax.random.fold_in(_gk, 3), (40000,), 0, 1250, jnp.int32)
        _o = jnp.argsort(dst, stable=True)
        src = src[_o]
        dst = dst[_o]
        return (x, src, dst)
    x, src, dst = _rec_inputs()

    def _L0_gnn_setup():
        import jax, jax.numpy as jnp
        import numpy as np
        N_NODES = 6250
        N_EDGES = 50000
        IN_DIM = 512
        OUT_DIM = 512
        key = jax.random.key(seed)
        k1, k2, k3, k4 = jax.random.split(key, 4)
        x = jax.random.normal(k1, (N_NODES, IN_DIM), dtype=jnp.float32)
        edge_index = jax.random.randint(k2, (2, N_EDGES), 0, N_NODES, dtype=jnp.int64)
        W = jax.random.normal(k3, (OUT_DIM, IN_DIM), dtype=jnp.float32) / np.sqrt(IN_DIM)
        b = jax.random.normal(k4, (OUT_DIM,), dtype=jnp.float32) * 0.01
        return {'x': x, 'edge_index': edge_index, 'W': W, 'b': b}
    _L0_gnn_all = _L0_gnn_setup()
    _L0_gnn_in = {k: v for k, v in _L0_gnn_all.items() if k in ('W', 'b')}
    del _L0_gnn_all

    def _L0_ffn_setup():
        import jax, jax.numpy as jnp
        import numpy as np
        B, T, D = (4, 1024, 512)
        E, F, CAP = (8, 256, 512)
        key = jax.random.key(seed)
        ks = jax.random.split(key, 6)
        s = 0.02
        return {'x': jax.random.normal(ks[0], (B, T, D), dtype=jnp.float32), 'Wr': jax.random.normal(ks[1], (D, E), dtype=jnp.float32) * s, 'W1': jax.random.normal(ks[2], (E, D, F), dtype=jnp.float32) * s, 'b1': jax.random.normal(ks[3], (E, F), dtype=jnp.float32) * s, 'W2': jax.random.normal(ks[4], (E, F, D), dtype=jnp.float32) * s, 'b2': jax.random.normal(ks[5], (E, D), dtype=jnp.float32) * s}
    _L0_ffn_all = _L0_ffn_setup()
    _L0_ffn_in = {k: v for k, v in _L0_ffn_all.items() if k in ('Wr', 'W1', 'b1', 'W2', 'b2')}
    del _L0_ffn_all
    return {'x': x, 'src': src, 'dst': dst, 'L0_gnn_W': _L0_gnn_in['W'], 'L0_gnn_b': _L0_gnn_in['b'], 'L0_ffn_Wr': _L0_ffn_in['Wr'], 'L0_ffn_W1': _L0_ffn_in['W1'], 'L0_ffn_b1': _L0_ffn_in['b1'], 'L0_ffn_W2': _L0_ffn_in['W2'], 'L0_ffn_b2': _L0_ffn_in['b2']}

def reference(x, src, dst, L0_gnn_W, L0_gnn_b, L0_ffn_Wr, L0_ffn_W1, L0_ffn_b1, L0_ffn_W2, L0_ffn_b2):
    import jax
    import jax.numpy as jnp

    def _L0_gnn_ref(x, edge_index, W, b):
        import jax, jax.numpy as jnp
        import numpy as np
        N_NODES = 6250
        N_EDGES = 50000
        IN_DIM = 512
        OUT_DIM = 512
        n = x.shape[0]
        loops = jnp.arange(n, dtype=edge_index.dtype)
        row = jnp.concatenate([edge_index[0], loops])
        col = jnp.concatenate([edge_index[1], loops])
        deg = jax.ops.segment_sum(jnp.ones(row.shape[0], dtype=x.dtype), row, num_segments=n)
        dis = jax.lax.rsqrt(deg)
        norm = dis[row] * dis[col]
        h = x @ W.T + b
        out = jax.ops.segment_sum(norm[:, None] * h[row], col, num_segments=n)
        return jax.nn.relu(out)

    def _L0_ffn_ref(x, Wr, W1, b1, W2, b2):
        import jax, jax.numpy as jnp
        import numpy as np
        B, T, D = (4, 1024, 512)
        E, F, CAP = (8, 256, 512)
        Bb, Tt, Dd = x.shape
        N = Bb * Tt
        C = min(CAP, N)
        x_flat = x.reshape(N, Dd)
        logits = x_flat @ Wr
        probs = jax.nn.softmax(logits, axis=0)
        vals, idx = jax.lax.top_k(probs.T, C)
        selected = x_flat[idx]
        h = jax.nn.gelu(jnp.einsum('ecd,edf->ecf', selected, W1) + b1[:, None, :], approximate=False)
        out_e = jnp.einsum('ecf,efd->ecd', h, W2) + b2[:, None, :]
        weighted = vals[..., None] * out_e
        output = jnp.zeros_like(x_flat).at[idx.reshape(-1)].add(weighted.reshape(-1, Dd))
        return output.reshape(Bb, Tt, Dd)
    edge_index = jnp.stack([src, dst])
    x = x + _L0_gnn_ref(_layernorm(x, axis=-1), edge_index, L0_gnn_W, L0_gnn_b)
    x = x + _L0_ffn_ref(_layernorm(x, axis=-1)[None], L0_ffn_Wr, L0_ffn_W1, L0_ffn_b1, L0_ffn_W2, L0_ffn_b2)[0]
    return x

_drawn_inputs = setup_inputs


def setup_inputs(seed=0):
    import zlib

    import numpy as np

    out = dict(_drawn_inputs(seed))
    spreads = {}
    factors = {'L0_gnn_b': 8.0,
     'L0_ffn_Wr': 8.0,
     'L0_ffn_W1': 8.0,
     'L0_ffn_b1': 52.506,
     'L0_ffn_W2': 8.0,
     'L0_ffn_b2': 64.0}
    for name, (base, spread) in spreads.items():
        noise = np.random.default_rng([zlib.crc32(name.encode()), seed]).standard_normal(out[name].shape)
        drawn = base * np.exp(spread * noise) if base else spread * noise
        out[name] = jnp.asarray(drawn.astype(out[name].dtype))
    for name, factor in factors.items():
        out[name] = (out[name] * factor).astype(out[name].dtype)
    return out
```

```python
from contextlib import ExitStack

import numpy as np

import concourse.bass as bass
from concourse import mybir

ALU = mybir.AluOpType
ACT = mybir.ActivationFunctionType
AX = mybir.AxisListType
F32 = mybir.dt.float32
F32R = mybir.dt.float32r
F16 = mybir.dt.float16
I32 = mybir.dt.int32

P = 128
EPS = 1e-5
ROUND = 12582912.0


def gnn_ffn(nc, x, src, dst, gnn_W, gnn_b, Wr, W1, b1, W2, b2, out):
    N, D = x.shape
    E = src.shape[0]
    NX, _, F = W1.shape
    KC = D // P
    FC = F // P
    TP = 125
    T = N // TP
    CAP = min(512, N)
    ROW = E // TP

    WIN = 10
    NW = N // WIN
    HC = 3
    SLOT = HC * P
    NCH = NW * HC
    NB = 5
    WB = NW // NB
    CB = WB * HC
    GW = 5
    KEYS = WIN + 2
    NK = T * WIN
    SETS = [(0, 3), (3, 5)]
    HSCALE = 16384.0
    G16 = 16
    ROUNDS = 7
    SPLIT = [(0, 120), (120, TP)]
    TG = [(0, 4), (4, 8), (8, 10)]
    assert T * TP == N and TP * ROW == E and NX * G16 == P and NW <= P and NB * WB == NW

    with ExitStack() as ctx:
        def sb(name, shape, dt):
            return ctx.enter_context(nc.sbuf_tensor(name, shape, dt))

        def sem(name):
            return ctx.enter_context(nc.semaphore(name))

        ident = sb("ident", [P, P], F32)
        ident16 = sb("ident16", [P, P], F16)
        ones = sb("ones", [P, P], F32)
        ones16 = sb("ones16", [P, P], F16)
        blk = sb("blk", [P, P], F32)
        win0 = sb("win0", [P, 1], F32)
        rowid = sb("rowid", [P, 1], F32)
        jcol = sb("jcol", [P, 3], F32)
        dst_e = sb("dst_e", [TP, ROW], I32)
        src_e = sb("src_e", [TP, ROW], I32)
        diag16 = sb("diag16", [TP, TP], F16)
        sm = sb("sm", [P, 16], F32)
        smi = sb("smi", [P, 4], I32)
        junk = sb("junk", [P, 1], F32)
        keyM = sb("keyM", [P, NCH + 1], F16)
        keyN = sb("keyN", [P, NCH + 1], F16)
        bn = sb("bn", [TP, T, 6], F32)
        mv = sb("mv", [TP, T, 2], F32)
        rstd = sb("rstd", [TP, 3, T], F32)
        nmr = sb("nmr", [TP, T], F32)
        wsc = sb("wsc", [P, 8, KC], F32)
        gb4 = sb("gb4", [KC, P], F32)
        degp = sb("degp", [TP, T, NB * 2], F32)
        dis = sb("dis", [TP, 4, T], F32)
        tot = sb("tot", [TP, 2], F32)
        flag = sb("flag", [1, 2], I32)
        bn2 = sb("bn2", [TP, 2, 6], F32)
        mv2 = sb("mv2", [TP, T, 2], F32)
        rs2 = sb("rs2", [TP, 4, T], F32)
        b1row = sb("b1row", [NX * FC, P], F32)
        b1col = sb("b1col", [P, NX * FC], F32)
        sel = sb("sel", [P, 16], F32)
        cnt = sb("cnt", [P, ROUNDS, 4], F32)
        lows = sb("lows", [P, ROUNDS + 1, 2], F32)
        wtok = sb("wtok", [TP, T, NX], F32)
        inv_bc = sb("inv_bc", [TP, D], F32)
        onesr = sb("onesr", [1, P], F32R)
        brow = sb("brow", [1, 2, D], F32R)

        base = (nc.sbuf_base + 63) // 64 * 64
        plan = {}

        def at(name, shape, dt, off):
            size = int(np.prod(shape[1:])) * (2 if dt == F16 else 4)
            plan[name] = (off, off + size)
            return nc.alloc_sbuf_tensor_at(name, shape, dt, offset=base + off)

        def end(name):
            return (plan[name][1] + 63) // 64 * 64

        AT = at("AT", [P, T, N + 6], F16, 0)
        HB = at("HB", [TP, T, D], F32, end("AT"))
        XNh = at("XNh", [P, 2, KC, TP], F32R, end("HB"))
        XNl = at("XNl", [P, 2, KC, TP], F32R, end("XNh"))
        WTh = at("WTh", [P, KC, D], F32R, end("XNl"))
        WTl = at("WTl", [P, KC, D], F32R, end("WTh"))
        OHM = at("OHM", [P, P, NCH], F16, end("WTl"))
        OHN = at("OHN", [P, 2, NK, CB], F16, end("OHM"))
        Wn = at("Wn", [P, KC, D], F32, plan["OHN"][0])
        Wsq = at("Wsq", [P, D], F32, end("Wn"))
        grow = at("grow", [TP, ROW], I32, end("Wsq"))
        grow16 = at("grow16", [TP, ROW], F16, end("grow"))
        gd = at("gd", [NW, SLOT], I32, end("grow16"))
        gs = at("gs", [NW, SLOT], I32, end("gd"))
        ek = at("ek", [NW, 4, SLOT], F32, end("gs"))
        ek16 = at("ek16", [NW, 2, SLOT], F16, end("ek"))
        dscale = at("dscale", [P, 2, KC, P], F32, end("ek16"))
        cmp16 = at("cmp16", [TP, ROW], F16, end("dscale"))
        assert end("cmp16") <= end("OHN")
        HDh = at("HDh", [TP, T, D], F16, plan["XNh"][0])
        HDl = at("HDl", [TP, T, D], F16, end("HDh"))
        assert end("HDl") <= plan["OHM"][0]
        AT2 = at("AT2", [P, T, N + 6], F16, plan["OHN"][0])
        dst_f = at("dst_f", [TP, ROW], F32, plan["OHM"][0])
        src_f = at("src_f", [TP, ROW], F32, end("dst_f"))
        srcq_f = at("srcq_f", [TP, ROW], F32, end("src_f"))
        iota_n = at("iota_n", [TP, N], F32, end("srcq_f"))
        ohs = at("ohs", [TP, 2, P], F16, end("iota_n"))
        ohd = at("ohd", [TP, 2, N // 5], F16, end("ohs"))
        atp = at("atp", [TP, N // 5], F32, end("ohd"))
        X1 = at("X1", [TP, T, D], F32, plan["OHM"][0])
        XTh = at("XTh", [P, KC, N], F32R, end("X1"))
        XTl = at("XTl", [P, KC, N], F32R, end("XTh"))
        xn2 = at("xn2", [TP, 2, D], F32, end("XTl"))
        WrN = at("WrN", [P, KC, NX], F32, end("xn2"))
        Wrh = at("Wrh", [P, KC, NX, G16], F32R, end("WrN"))
        Wrl = at("Wrl", [P, KC, NX, G16], F32R, end("Wrh"))
        LG = at("LG", [P, N], F32, end("Wrl"))
        b2z = at("b2z", [P, D], F32, end("LG"))
        W1n = at("W1n", [P, 2, KC, F], F32, end("b2z"))
        W2n = at("W2n", [P, 2, FC, D], F32, end("W1n"))
        assert end("W2n") <= plan["OHN"][0], (end("W2n"), plan["OHN"][0])
        W1h, W1l, W2h, W2l = [], [], [], []
        for n, off in enumerate((plan["HB"][0], plan["OHN"][0])):
            W1h.append(at(f"W1h{n}", [P, KC, F], F32R, off))
            W1l.append(at(f"W1l{n}", [P, KC, F], F32R, end(f"W1h{n}")))
            W2h.append(at(f"W2h{n}", [P, FC, D], F32R, end(f"W1l{n}")))
            W2l.append(at(f"W2l{n}", [P, FC, D], F32R, end(f"W2h{n}")))
        Hh = at("Hh", [P, 2, FC, N], F32R, 0)
        Hl = at("Hl", [P, 2, FC, N], F32R, plan["XNh"][0])
        HG = at("HG", [P, 2, 512], F32, end("W2l0"))
        assert end("Hh") <= plan["HB"][0] and end("Hl") <= plan["OHM"][0] and end("HG") <= plan["XNh"][0]
        EX = at("EX", [P, N], F32, end("W2l1"))
        GE = at("GE", [P, N], F32, end("EX"))
        assert end("GE") <= end("OHN"), (end("GE"), end("OHN"))
        CL = at("CL", [P, N], F32, end("Hh"))
        assert end("CL") <= plan["HB"][0]

        banks = [ctx.enter_context(nc.psum_tensor(f"bank{i}", [P, 512], F32)) for i in range(3)]
        TR = banks[0:2]
        psX = ctx.enter_context(nc.psum_tensor("psX", [P, 3, 512], F32))
        psY = ctx.enter_context(nc.psum_tensor("psY", [P, 2, 512], F32))
        H = [banks[2], psY[:, 0, :]]
        O4 = [banks[0], banks[1], banks[2], psY[:, 0, :]]
        psS = psY[:, 1, :]
        psS16 = psS.bitcast(F16)
        AB = [psX, psY]

        s_dst = sem("s_dst")
        s_x = [sem(f"s_x{i}") for i in range(5)]
        s_W = sem("s_W")
        s_gb = sem("s_gb")
        s_ident = sem("s_ident")
        s_const = sem("s_const")
        s_link = sem("s_link")
        s_diag = sem("s_diag")
        s_rowps = sem("s_rowps")
        s_rr = sem("s_rr")
        s_grow = sem("s_grow")
        s_start = sem("s_start")
        s_gath = sem("s_gath")
        s_ek = sem("s_ek")
        s_kps = sem("s_kps")
        s_key = sem("s_key")
        s_ssq = sem("s_ssq")
        s_gbT = sem("s_gbT")
        s_babs = sem("s_babs")
        s_wroot = sem("s_wroot")
        s_wscale = sem("s_wscale")
        s_var = sem("s_var")
        s_std = sem("s_std")
        s_nmr = sem("s_nmr")
        s_xn = sem("s_xn")
        s_tr = sem("s_tr")
        s_hi = sem("s_hi")
        s_lo = sem("s_lo")
        s_bc = sem("s_bc")
        s_bcv = sem("s_bcv")
        s_h = sem("s_h")
        s_hb = sem("s_hb")
        s_pad = sem("s_pad")
        s_blk = sem("s_blk")
        s_m = sem("s_m")
        s_n = sem("s_n")
        s_set = sem("s_set")
        s_at = sem("s_at")
        s_src = sem("s_src")
        s_gsrc = sem("s_gsrc")
        s_gp = sem("s_gp")
        s_gend = sem("s_gend")
        s_tot = sem("s_tot")
        s_totps = sem("s_totps")
        s_flag = sem("s_flag")
        s_giota = sem("s_giota")
        s_goh = sem("s_goh")
        s_gmm = sem("s_gmm")
        s_gev = sem("s_gev")
        s_counts = sem("s_counts")
        s_droot = sem("s_droot")
        s_dis = sem("s_dis")
        s_hdh = sem("s_hdh")
        s_hdl = sem("s_hdl")
        s_x1 = [sem(f"s_x1{i}") for i in range(5)]
        s_agg = sem("s_agg")
        s_res = sem("s_res")
        s_var2 = sem("s_var2")
        s_std2 = sem("s_std2")
        s_nmr2 = sem("s_nmr2")
        s_xn2 = sem("s_xn2")
        s_tr2 = sem("s_tr2")
        s_hi2 = sem("s_hi2")
        s_lo2 = sem("s_lo2")
        s_Wr = sem("s_Wr")
        s_b1 = sem("s_b1")
        s_b2 = sem("s_b2")
        s_b2z = sem("s_b2z")
        s_b1T = sem("s_b1T")
        s_b1c = sem("s_b1c")
        s_wrs = sem("s_wrs")
        s_lgp = sem("s_lgp")
        s_lg = sem("s_lg")
        s_max = sem("s_max")
        s_exp = sem("s_exp")
        s_ind = sem("s_ind")
        s_m16 = sem("s_m16")
        s_w = sem("s_w")
        s_wT = sem("s_wT")
        s_wtok = sem("s_wtok")
        s_b2p = sem("s_b2p")
        s_b2a = sem("s_b2a")
        s_w1n = [sem("s_w1n0"), sem("s_w1n1")]
        s_w2n = [sem("s_w2n0"), sem("s_w2n1")]
        s_w1h = sem("s_w1h")
        s_w2h = sem("s_w2h")
        s_w1l = sem("s_w1l")
        s_w2l = sem("s_w2l")
        s_mm1 = sem("s_mm1")
        s_gelu = sem("s_gelu")
        s_hh = sem("s_hh")
        s_hl = sem("s_hl")
        s_mm2 = sem("s_mm2")
        s_acc = sem("s_acc")
        s_out = sem("s_out")
        sets = len(SETS)
        PIECES = [(f, a, b) for f in range(FC) for a, b in ((0, 500), (500, 1000), (1000, N))]
        NP = len(PIECES)

        x_v = x.rearrange("(t p) d -> p t d", p=TP)
        out_v = out.rearrange("(t p) d -> p t d", p=TP)
        dst_v = dst.rearrange("(r c) -> r c", c=ROW)
        src_v = src.rearrange("(r c) -> r c", c=ROW)

        block = ctx.enter_context(nc.Block())

        @block.sync
        def _(sp):
            for a, b in SPLIT:
                sp.dma_start(dst_e[a:b, :], dst_v[a:b, :]).then_inc(s_dst, 16)
            for i in range(5):
                for a, b in SPLIT:
                    sp.dma_start(HB[a:b, 2 * i:2 * i + 2, :], x_v[a:b, 2 * i:2 * i + 2, :]).then_inc(s_x[i], 16)

            for a, b in SPLIT:
                sp.dma_start(src_e[a:b, :], src_v[a:b, :]).then_inc(s_src, 16)
            sp.dma_start(b1row[:], b1.rearrange("e (f p) -> (e f) p", p=P)).then_inc(s_b1, 16)
            sp.wait_ge(s_counts, 1)
            for i in range(5):
                for a, b in SPLIT:
                    sp.dma_start(X1[a:b, 2 * i:2 * i + 2, :], x_v[a:b, 2 * i:2 * i + 2, :]).then_inc(s_x1[i], 16)
                if i == 0:
                    sp.dma_start(WrN[:], Wr.rearrange("(c p) e -> p c e", p=P)).then_inc(s_Wr, 16)
            for e in range(NX):
                if e >= 2:
                    sp.wait_ge(s_w1l, e - 1)
                    sp.wait_ge(s_w1h, e - 1)
                sp.dma_start(W1n[:, e % 2, :, :], W1[e].rearrange("(c p) f -> p c f", p=P)).then_inc(s_w1n[e % 2], 16)
                if e >= 2:
                    sp.wait_ge(s_w2l, e - 1)
                    sp.wait_ge(s_w2h, e - 1)
                sp.dma_start(W2n[:, e % 2, :, :], W2[e].rearrange("(c p) d -> p c d", p=P)).then_inc(s_w2n[e % 2], 16)
                if e == 0:
                    sp.wait_ge(s_b2z, 1)
                    sp.dma_start(b2z[0:P:G16, :], b2).then_inc(s_b2, 16)
            for i in range(5):
                sp.wait_ge(s_acc, (NX - 1) * T + 2 * i + 2)
                for a, b in SPLIT:
                    sp.dma_start(out_v[a:b, 2 * i:2 * i + 2, :], X1[a:b, 2 * i:2 * i + 2, :]).then_inc(s_out, 16)
            sp.wait_ge(s_out, 16 * 10)
            sp.wait_ge(s_src, 32)

        @block.gpsimd
        def _(pool):
            pool.memset(ident[:], 0.0).then_inc(s_ident, 1)
            pool.memset(ones16[:], 1.0).then_inc(s_const, 1)
            pool.wait_ge(s_ident, 1)
            pool.affine_select(out=ident[:], in_=ident[:], compare_op=ALU.not_equal, fill=1.0, base=0,
                               pattern=[[-1, P]], channel_multiplier=1).then_inc(s_ident, 1)
            pool.iota(win0[:], pattern=[[0, 1]], base=0, channel_multiplier=WIN,
                      allow_small_or_imprecise_dtypes=True).then_inc(s_const, 1)
            pool.memset(ones[:], 1.0).then_inc(s_const, 1)
            pool.memset(OHM[:, TP:P, :].rearrange("p a c -> p (a c)"), 0.0).then_inc(s_pad, 1)
            pool.wait_ge(s_rr, 1)
            pool.indirect_dma_start(out=grow[:], out_offset=None, in_=dst_v,
                                    in_offset=bass.IndirectOffsetOnAxis(ap=smi[0:TP, 0:1], axis=0)
                                    ).then_inc(s_grow, 16)
            pool.wait_ge(s_start, 1)
            for lst, to in ((dst, gd), (src, gs)):
                pool.indirect_dma_start(out=to[:], out_offset=None, in_=lst.rearrange("(a n) -> a n", a=1),
                                        in_offset=bass.IndirectOffsetOnAxis(ap=smi[0:NW, 1:2], axis=1)
                                        ).then_inc(s_gath, 16)

            pool.memset(blk[:], 1.0).then_inc(s_blk, 1)
            pool.iota(rowid[:], pattern=[[0, 1]], base=0, channel_multiplier=1,
                      allow_small_or_imprecise_dtypes=True).then_inc(s_blk, 1)
            blk_v = blk[:].rearrange("p (g j) -> p g j", j=G16)
            pool.wait_ge(s_blk, 2)
            pool.affine_select(out=blk_v, in_=blk_v, compare_op=ALU.is_ge, fill=0.0, base=0,
                               pattern=[[-G16, NX], [0, G16]], channel_multiplier=1).then_inc(s_blk, 1)
            pool.wait_ge(s_blk, 3)
            pool.affine_select(out=blk_v, in_=blk_v, compare_op=ALU.is_ge, fill=0.0, base=G16 - 1,
                               pattern=[[G16, NX], [0, G16]], channel_multiplier=-1).then_inc(s_blk, 1)

            pool.wait_ge(s_flag, 1)
            general = pool.value_load(flag[0:1, 0:1], min_val=0, max_val=1)
            with pool.If(general):
                pool.iota(iota_n[:], pattern=[[1, N]], base=0, channel_multiplier=0,
                          allow_small_or_imprecise_dtypes=True).then_inc(s_giota, 1)

            pool.wait_ge(s_counts, 1)
            pool.memset(b2z[:], 0.0).then_inc(s_b2z, 1)

            def low(to, full, high, done):
                pool.tensor_tensor(to, full, high.bitcast(F32), ALU.subtract).then_inc(done, 1)

            def low_w1(e):
                if e >= 2:
                    pool.wait_ge(s_mm1, NP * (e - 1))
                pool.wait_ge(s_w1h, e + 1)
                pool.wait_ge(s_w1n[e % 2], 16 * (e // 2 + 1))
                low(W1l[e % 2][:], W1n[:, e % 2, :, :], W1h[e % 2][:], s_w1l)

            def low_w2(e):
                if e >= 2:
                    pool.wait_ge(s_mm2, T * (e - 1))
                pool.wait_ge(s_w2h, e + 1)
                pool.wait_ge(s_w2n[e % 2], 16 * (e // 2 + 1))
                low(W2l[e % 2][:], W2n[:, e % 2, :, :], W2h[e % 2][:], s_w2l)

            low_w1(0)
            low_w2(0)
            low_w1(1)
            for e in range(NX):
                for i, (f, a, b) in enumerate(PIECES):
                    pool.wait_ge(s_hh, e * NP + i + 1)
                    if e >= 2:
                        pool.wait_ge(s_mm2, T * (e - 1))
                    low(Hl[:, e % 2, f, a:b], HG[:, i % 2, 0:b - a], Hh[:, e % 2, f, a:b], s_hl)
                if e + 1 < NX:
                    low_w2(e + 1)
                if e + 2 < NX:
                    low_w1(e + 2)

        @block.scalar
        def _(act):
            act.dma_start(Wn[:], gnn_W.rearrange("(c p) i -> p c i", p=P)).then_inc(s_W, 16)
            act.dma_start(gb4[:], gnn_b.rearrange("(c p) -> c p", p=P)).then_inc(s_gb, 16)
            act.wait_ge(s_W, 16)
            for c in range(KC):
                if c:
                    act.wait_ge(s_ssq, c)
                act.activation(Wsq[:], Wn[:, c, :], ACT.Square, accum_out=wsc[:, 0, c:c + 1]).then_inc(s_ssq, 1)
            act.wait_ge(s_ssq, KC)
            act.activation(wsc[:, 1, :], wsc[:, 0, :], ACT.Sqrt, scale=float(D)).then_inc(s_wroot, 1)

            def root(g):
                act.wait_ge(s_var, g + 1)
                act.activation(rstd[:, 1, 5 * g:5 * g + 5], rstd[:, 0, 5 * g:5 * g + 5], ACT.Sqrt).then_inc(s_std, 1)

            def norm(t):
                act.wait_ge(s_nmr, t // 5 + 1)
                act.activation(HB[:, t, :], HB[:, t, :], ACT.Identity, bias=nmr[:, t:t + 1],
                               scale=rstd[:, 2, t:t + 1]).then_inc(s_xn, 1)

            def high_w(c):
                act.wait_ge(s_tr, c + 1)
                act.activation(WTh[:, c, :], TR[c % 2][:], ACT.Copy).then_inc(s_hi, 1)

            def high_x(t):
                act.wait_ge(s_tr, KC + t + 1)
                if t >= 2:
                    act.wait_ge(s_h, t - 1)
                act.activation(XNh[:, t % 2, :, :].rearrange("p a c -> p (a c)"), TR[t % 2][:, 0:KC * TP],
                               ACT.Copy).then_inc(s_hi, 1)

            def hidden(t):
                act.wait_ge(s_h, t + 1)
                act.activation(HB[:, t, :], H[t % 2][0:TP, :], ACT.Copy).then_inc(s_hb, 1)

            root(0)
            for c in range(KC):
                high_w(c)
            for t in range(3):
                norm(t)
            for t in range(T):
                high_x(t)
                if t == 1:
                    root(1)
                if t + 3 < T:
                    norm(t + 3)
                if t >= 1:
                    hidden(t - 1)
            hidden(T - 1)

            for b in range(NB):
                for k, (g0, g1) in enumerate(SETS):
                    act.wait_ge(s_set, 2 * b + k + 1)
                    ps = AB[k][0:TP, :, 0:GW * NK].rearrange("p g (w q d) -> p q g w d", q=T, d=WIN)
                    d0 = (b * 5 + g0) * GW * WIN
                    for q in range(T):
                        to = AT[0:TP, q, d0:d0 + (g1 - g0) * GW * WIN].rearrange("p (g w d) -> p g w d", w=GW, d=WIN)
                        last = act.activation(to, ps[:, q], ACT.Copy, accum_out=degp[:, q, 2 * b + k:2 * b + k + 1])
                    last.then_inc(s_at, 1)

            act.wait_ge(s_counts, 1)
            act.activation(dis[:, 2, :], dis[:, 1, :], ACT.Sqrt).then_inc(s_droot, 1)
            act.wait_ge(s_dis, 1)
            for t in range(T):
                act.activation(HDh[:, t, :], HB[:, t, :], ACT.Copy, scale=dis[:, 3, t:t + 1]).then_inc(s_hdh, 1)

            def high_w1(e):
                if e >= 2:
                    act.wait_ge(s_mm1, NP * (e - 1))
                elif e == 0:
                    act.wait_ge(s_hdl, T)
                else:
                    act.wait_ge(s_agg, T)
                act.wait_ge(s_w1n[e % 2], 16 * (e // 2 + 1))
                act.activation(W1h[e % 2][:], W1n[:, e % 2, :, :], ACT.Copy).then_inc(s_w1h, 1)

            def high_w2(e):
                if e >= 2:
                    act.wait_ge(s_mm2, T * (e - 1))
                act.wait_ge(s_w2n[e % 2], 16 * (e // 2 + 1))
                act.activation(W2h[e % 2][:], W2n[:, e % 2, :, :], ACT.Copy).then_inc(s_w2h, 1)

            def root2(t):
                act.wait_ge(s_var2, t + 1)
                act.activation(rs2[:, 1, t:t + 1], rs2[:, 0, t:t + 1], ACT.Sqrt).then_inc(s_std2, 1)

            def norm2(t):
                act.wait_ge(s_nmr2, t + 1)
                if t >= 2:
                    act.wait_ge(s_tr2, t - 1)
                act.activation(xn2[:, t % 2, :], X1[:, t, :], ACT.Identity, bias=rs2[:, 3, t:t + 1],
                               scale=rs2[:, 2, t:t + 1]).then_inc(s_xn2, 1)

            def high_x2(t):
                act.wait_ge(s_tr2, t + 1)
                act.activation(XTh[:, :, t * TP:(t + 1) * TP],
                               TR[t % 2][:, 0:KC * TP].rearrange("p (c n) -> p c n", c=KC), ACT.Copy).then_inc(s_hi2, 1)

            for t in range(T):
                root2(t)
                norm2(t)
                if t == 4:
                    high_w1(0)
                if t == 5:
                    high_w2(0)
                if t >= 1:
                    high_x2(t - 1)
            high_x2(T - 1)
            for g, (t0, t1) in enumerate(TG):
                act.wait_ge(s_lgp, g + 1)
                act.activation(LG[:, t0 * TP:t1 * TP], psX[:, g, 0:(t1 - t0) * TP], ACT.Copy).then_inc(s_lg, 1)
            act.wait_ge(s_max, 1)
            act.activation(EX[:], LG[:], ACT.Exp, bias=sel[:, 1:2], accum_out=sel[:, 2:3]).then_inc(s_exp, 1)
            high_w1(1)

            act.wait_ge(s_b1c, 1)
            for e in range(NX):
                for i, (f, a, b) in enumerate(PIECES):
                    n = e * NP + i
                    act.wait_ge(s_mm1, n + 1)
                    if n >= 2:
                        act.wait_ge(s_hl, n - 1)
                    if e >= 2:
                        act.wait_ge(s_mm2, T * (e - 1))
                    act.activation(HG[:, i % 2, 0:b - a], psX[:, i % 3, 0:b - a], ACT.Gelu,
                                   bias=b1col[:, e * FC + f:e * FC + f + 1]).then_inc(s_gelu, 1)
                    act.wait_ge(s_gelu, n + 1)
                    act.activation(Hh[:, e % 2, f, a:b], HG[:, i % 2, 0:b - a], ACT.Copy).then_inc(s_hh, 1)
                if e + 1 < NX:
                    high_w2(e + 1)
                if e + 2 < NX:
                    high_w1(e + 2)

        @block.vector
        def _(dve):
            chain = [0]

            def link(ins):
                chain[0] += 1
                ins.then_inc(s_link, 1)
                dve.wait_ge(s_link, chain[0])

            dve.wait_ge(s_ident, 2)
            link(dve.tensor_copy(ident16[:], ident[:]))
            dve.wait_ge(s_dst, 32)
            dve.tensor_scalar(diag16[:], ident16[0:TP, 0:TP], dst_e[:, 0:1], None, ALU.mult).then_inc(s_diag, 1)

            def stats(t):
                dve.wait_ge(s_x[t // 2], 32)
                link(dve.bn_stats(bn[:, t, :], HB[:, t, :]))
                link(dve.bn_aggr(mv[:, t, :], bn[:, t, :]))

            def variances(g):
                a, b = 5 * g, 5 * g + 5
                dve.tensor_scalar(rstd[:, 0, a:b], mv[:, a:b, 1], EPS, None, ALU.add).then_inc(s_var, 1)

            def scales(g):
                a, b = 5 * g, 5 * g + 5
                dve.wait_ge(s_std, g + 1)
                link(dve.reciprocal(rstd[:, 2, a:b], rstd[:, 1, a:b]))
                dve.scalar_tensor_tensor(nmr[:, a:b], mv[:, a:b, 0], -1.0, rstd[:, 2, a:b], ALU.mult,
                                         ALU.mult).then_inc(s_nmr, 1)

            dve.wait_ge(s_rowps, 1)
            dve.wait_ge(s_const, 3)
            link(dve.tensor_scalar(cmp16[0:TP, 0:TP], psS[0:TP, 0:TP], win0[0:TP, :], None, ALU.is_lt, ALU.add,
                                   accum_out=sm[0:TP, 0:1]))
            link(dve.tensor_scalar(sm[0:TP, 1:2], sm[0:TP, 0:1], -1.0, 0.0, ALU.add, ALU.max))
            dve.tensor_copy(smi[0:TP, 0:1], sm[0:TP, 1:2]).then_inc(s_rr, 1)
            for t in range(2):
                stats(t)
            dve.wait_ge(s_grow, 16)
            link(dve.tensor_copy(grow16[:], grow[:]))
            link(dve.tensor_scalar(cmp16[:], grow16[:], win0[0:TP, :], None, ALU.is_lt, ALU.add,
                                   accum_out=sm[0:TP, 2:3]))
            link(dve.scalar_tensor_tensor(sm[0:TP, 3:4], sm[0:TP, 1:2], float(ROW), sm[0:TP, 2:3], ALU.mult, ALU.add))
            link(dve.tensor_scalar(sm[0:TP, 4:5], sm[0:TP, 3:4], float(E - SLOT), None, ALU.min))
            dve.tensor_copy(smi[0:NW, 1:2], sm[0:NW, 4:5]).then_inc(s_start, 1)

            dve.wait_ge(s_gbT, 1)
            link(dve.tensor_scalar(wsc[:, 2, :], psS[:, 256:256 + KC], -1.0, None, ALU.mult))
            link(dve.tensor_tensor(wsc[:, 3, :], psS[:, 256:256 + KC], wsc[:, 2, :], ALU.max))
            dve.wait_ge(s_wroot, 1)
            link(dve.scalar_tensor_tensor(wsc[:, 4, :], wsc[:, 1, :], 1e-30, wsc[:, 3, :], ALU.add, ALU.add))
            link(dve.tensor_scalar(wsc[:, 5, :], wsc[:, 4, :], 1.0 / HSCALE, None, ALU.mult))
            link(dve.reciprocal(wsc[:, 6, :], wsc[:, 5, :]))
            link(dve.scalar_tensor_tensor(wsc[:, 7, :], wsc[:, 2, :], -1.0, wsc[:, 6, :], ALU.mult, ALU.mult))
            for c in range(KC):
                dve.tensor_scalar(Wn[:, c, :], Wn[:, c, :], wsc[:, 6, c:c + 1], None, ALU.mult).then_inc(s_wscale, 1)
            for c in range(KC):
                dve.tensor_scalar(dscale[:, 0, c, :], ident[:], wsc[:, 7, c:c + 1], None, ALU.mult)
                last = dve.tensor_scalar(dscale[:, 1, c, :], ident[:], wsc[:, 5, c:c + 1], None, ALU.mult)
            last.then_inc(s_wscale, 1)
            for t in range(2, 5):
                stats(t)
            variances(0)

            dve.wait_ge(s_gath, 32)
            link(dve.tensor_scalar(ek[:, 0, :], gd[:], win0[0:NW, :], None, ALU.subtract))
            link(dve.tensor_scalar(ek[:, 0, :], ek[:, 0, :], -1.0, float(WIN), ALU.max, ALU.min))
            link(dve.tensor_scalar(ek[:, 1, :], gs[:], 1.0 / TP, 0.5 / TP - 0.5, ALU.mult, ALU.add))
            link(dve.tensor_scalar(ek[:, 2, :], ek[:, 1, :], ROUND, -ROUND, ALU.add, ALU.add))
            dve.scalar_tensor_tensor(ek16[:, 0, :], ek[:, 2, :], -float(TP), gs[:], ALU.mult, ALU.add).then_inc(s_ek, 1)
            dve.scalar_tensor_tensor(ek16[:, 1, :], ek[:, 2, :], float(KEYS), ek[:, 0, :], ALU.mult,
                                     ALU.add).then_inc(s_ek, 1)
            scales(0)

            def low_w(c):
                dve.wait_ge(s_hi, c + 1)
                dve.tensor_tensor(WTl[:, c, :], TR[c % 2][:], WTh[:, c, :].bitcast(F32), ALU.subtract).then_inc(s_lo, 1)

            def low_x(t):
                dve.wait_ge(s_hi, KC + t + 1)
                dve.tensor_tensor(XNl[:, t % 2, :, :].rearrange("p a c -> p (a c)"), TR[t % 2][:, 0:KC * TP],
                                  XNh[:, t % 2, :, :].rearrange("p a c -> p (a c)").bitcast(F32),
                                  ALU.subtract).then_inc(s_lo, 1)

            for c in range(KC):
                low_w(c)
            dve.wait_ge(s_bc, 1)
            dve.tensor_copy(onesr[:], ones[0:1, :])
            link(dve.tensor_copy(brow[:, 0, :], H[0][0:1, :]))
            dve.tensor_tensor(brow[:, 1, :], H[0][0:1, :], brow[:, 0, :].bitcast(F32), ALU.subtract).then_inc(s_bcv, 1)
            dve.tensor_copy(inv_bc[:], H[1][0:TP, :]).then_inc(s_bcv, 1)
            for t in range(5, T):
                stats(t)
            variances(1)
            low_x(0)
            dve.wait_ge(s_kps, 1)
            for k, to in ((0, keyM), (1, keyN)):
                last = dve.tensor_copy(to[:, 0:NCH].rearrange("p (w h) -> p h w", h=HC),
                                       psS16[:, k * HC * (NW + 1):(k + 1) * HC * (NW + 1)].rearrange(
                                           "p (h w) -> p h w", h=HC)[:, :, 0:NW])
            link(last)
            scales(1)

            done = 1
            for j in range(TP):
                dve.tensor_scalar(OHM[:, j, :], keyM[:, 0:NCH], float(j), None, ALU.is_equal).then_inc(s_m, 1)
                if j % 12 == 11 and done < T:
                    low_x(done)
                    done += 1
            for b in range(NB):
                if b >= 2:
                    dve.wait_ge(s_set, 2 * b - 2)
                for n in range(NK):
                    key = float(n // WIN * KEYS + n % WIN)
                    last = dve.tensor_scalar(OHN[:, b % 2, n, :], keyN[:, b * CB:(b + 1) * CB], key, None, ALU.is_equal)
                last.then_inc(s_n, 1)

            dve.wait_ge(s_at, 2 * NB)
            link(dve.tensor_reduce(dis[:, 0, :], degp[:], AX.X, ALU.add))
            dve.tensor_reduce(tot[:, 0:1], dis[:, 0, :], AX.X, ALU.add).then_inc(s_tot, 1)
            link(dve.tensor_scalar(dis[:, 1, :], dis[:, 0, :], 1.0, None, ALU.add))
            for t in range(T):
                own = AT[0:TP, t, t * TP:(t + 1) * TP]
                last = dve.tensor_tensor(own, own, ident16[0:TP, 0:TP], ALU.add)
            link(last)
            dve.wait_ge(s_totps, 1)
            dve.tensor_scalar(flag[:, 0:1], psS[0:1, 0:1], float(E), None, ALU.not_equal).then_inc(s_flag, 1)
            dve.wait_ge(s_flag, 1)
            general = dve.value_load(flag[0:1, 0:1], min_val=0, max_val=1)
            with dve.If(general):
                dve.wait_ge(s_src, 32)
                dve.wait_ge(s_giota, 1)
                dve.tensor_copy(dst_f[:], dst_e[:]).then_inc(s_gev, 1)
                dve.tensor_copy(src_f[:], src_e[:]).then_inc(s_gsrc, 1)
                DC = N // 5
                with dve.Fori(0, T) as q:
                    dve.wait_ge(s_gsrc, q + 1)
                    dve.wait_ge(s_gmm, q * (5 * ROW // 2) + 1)
                    dve.tensor_scalar(srcq_f[:], src_f[:], iota_n[:, bass.ds(q * TP, 1)], None,
                                      ALU.subtract).then_inc(s_gsrc, 1)
                    dve.wait_ge(s_gsrc, q + 2)
                    dve.tensor_copy(junk[:, 0:1], win0[:])
                    with dve.Fori(0, 5) as d:
                        with dve.Fori(0, ROW // 2) as c:
                            step = (q * 5 + d) * (ROW // 2) + c
                            dve.wait_ge(s_gmm, step + 1)
                            for k in range(2):
                                dve.tensor_scalar(ohs[:, k, 0:TP], iota_n[:, 0:TP], srcq_f[:, bass.ds(c * 2 + k, 1)],
                                                  None, ALU.is_equal)
                                last = dve.tensor_scalar(ohd[:, k, :], iota_n[:, bass.ds(d * DC, DC)],
                                                         dst_f[:, bass.ds(c * 2 + k, 1)], None, ALU.is_equal)
                            last.then_inc(s_goh, 1)
                        group = q * 5 + d
                        dve.wait_ge(s_gmm, (group + 1) * (ROW // 2) + 1)
                        dve.tensor_copy(atp[:], psS[0:TP, 0:DC]).then_inc(s_gp, 1)
                        dve.wait_ge(s_gp, group * 2 + 1)
                        part = AT[0:TP, bass.ds(q, 1), bass.ds(d * DC, DC)].rearrange("p a n -> p (a n)")
                        part2 = AT2[0:TP, bass.ds(q, 1), bass.ds(d * DC, DC)].rearrange("p a n -> p (a n)")
                        dve.tensor_copy(part, atp[:]).then_inc(s_gp, 1)
                        dve.wait_ge(s_gp, group * 2 + 2)
                        dve.tensor_tensor(part2, atp[:], part, ALU.subtract).then_inc(s_gev, 1)
                dve.wait_ge(s_gev, 5 * T + 1)
                for t in range(T):
                    own = AT2[0:TP, t, t * TP:(t + 1) * TP]
                    last = dve.tensor_tensor(own, own, ident16[0:TP, 0:TP], ALU.add)
                last.then_inc(s_gend, 1)
                dve.wait_ge(s_gend, 1)
                dve.tensor_reduce(dis[:, 0, :], AT[0:TP, :, 0:N], AX.X, ALU.add)
                dve.tensor_reduce(dis[:, 2, :], AT2[0:TP, :, 0:N], AX.X, ALU.add).then_inc(s_gend, 1)
                dve.wait_ge(s_gend, 2)
                dve.tensor_tensor(dis[:, 1, :], dis[:, 0, :], dis[:, 2, :], ALU.add).then_inc(s_gend, 1)
                dve.wait_ge(s_gend, 3)
            dve.tensor_copy(junk[:, 0:1], win0[:]).then_inc(s_counts, 1)

            dve.wait_ge(s_droot, 1)
            dve.reciprocal(dis[:, 3, :], dis[:, 2, :]).then_inc(s_dis, 1)
            dve.wait_ge(s_dis, 1)
            for t in range(T):
                dve.wait_ge(s_hdh, t + 1)
                dve.scalar_tensor_tensor(HDl[:, t, :], HB[:, t, :], dis[:, 3, t:t + 1], HDh[:, t, :], ALU.mult,
                                         ALU.subtract).then_inc(s_hdl, 1)

            dve.wait_ge(s_Wr, 16)
            wide = WrN[:].unsqueeze(3).to_broadcast([P, KC, NX, G16])
            link(dve.tensor_copy(Wrh[:], wide))
            dve.tensor_tensor(Wrl[:], wide, Wrh[:].bitcast(F32), ALU.subtract).then_inc(s_wrs, 1)
            dve.wait_ge(s_blk, 2)
            link(dve.tensor_scalar(jcol[:, 1:2], rowid[:], 1.0 / G16, 0.5 / G16 - 0.5, ALU.mult, ALU.add))
            link(dve.tensor_scalar(jcol[:, 2:3], jcol[:, 1:2], ROUND, -ROUND, ALU.add, ALU.add))
            link(dve.scalar_tensor_tensor(jcol[:, 0:1], jcol[:, 2:3], -float(G16), rowid[:], ALU.mult, ALU.add))

            def low_x2(t):
                dve.wait_ge(s_hi2, t + 1)
                to = XTl[:, :, t * TP:(t + 1) * TP]
                dve.tensor_tensor(to, TR[t % 2][:, 0:KC * TP].rearrange("p (c n) -> p c n", c=KC),
                                  XTh[:, :, t * TP:(t + 1) * TP].bitcast(F32), ALU.subtract).then_inc(s_lo2, 1)

            for t in range(T):
                dve.wait_ge(s_agg, t + 1)
                dve.wait_ge(s_x1[t // 2], 32)
                if t >= 2:
                    dve.wait_ge(s_tr2, t - 1)
                tmp = xn2[:, t % 2, :]
                dve.scalar_tensor_tensor(tmp, H[t % 2][0:TP, :], 0.0, inv_bc[:], ALU.max, ALU.mult).then_inc(s_res, 1)
                dve.wait_ge(s_res, t + 1)
                link(dve.scalar_tensor_tensor(X1[:, t, :], tmp, dis[:, 3, t:t + 1], X1[:, t, :], ALU.mult, ALU.add))
                link(dve.bn_stats(bn2[:, t % 2, :], X1[:, t, :]))
                link(dve.bn_aggr(mv2[:, t, :], bn2[:, t % 2, :]))
                dve.tensor_scalar(rs2[:, 0, t:t + 1], mv2[:, t, 1:2], EPS, None, ALU.add).then_inc(s_var2, 1)
                dve.wait_ge(s_std2, t + 1)
                link(dve.reciprocal(rs2[:, 2, t:t + 1], rs2[:, 1, t:t + 1]))
                dve.scalar_tensor_tensor(rs2[:, 3, t:t + 1], mv2[:, t, 0:1], -1.0, rs2[:, 2, t:t + 1], ALU.mult,
                                         ALU.mult).then_inc(s_nmr2, 1)
                if t >= 1:
                    low_x2(t - 1)
            low_x2(T - 1)
            dve.wait_ge(s_b1T, 1)
            dve.tensor_copy(b1col[:], psS[:, 256:256 + NX * FC]).then_inc(s_b1c, 1)

            dve.wait_ge(s_lg, len(TG))
            dve.tensor_reduce(sel[:, 0:1], LG[:], AX.X, ALU.max)
            link(dve.tensor_reduce(lows[:, 0, 0:1], LG[:], AX.X, ALU.min))
            dve.tensor_scalar(sel[:, 1:2], sel[:, 0:1], -1.0, None, ALU.mult).then_inc(s_max, 1)
            link(dve.tensor_tensor(sel[:, 3:4], sel[:, 0:1], lows[:, 0, 0:1], ALU.subtract))
            link(dve.scalar_tensor_tensor(sel[:, 4:5], lows[:, 0, 0:1], -1.0, sel[:, 0:1], ALU.mult, ALU.max))
            link(dve.tensor_scalar(sel[:, 4:5], sel[:, 4:5], 1e-6, 1e-30, ALU.mult, ALU.add))
            link(dve.scalar_tensor_tensor(sel[:, 5:6], sel[:, 3:4], 1.001, sel[:, 4:5], ALU.mult, ALU.add))
            link(dve.tensor_scalar(lows[:, 0, 1:2], sel[:, 5:6], 1.0 / G16, None, ALU.mult))
            for r in range(ROUNDS):
                link(dve.scalar_tensor_tensor(cnt[:, r, 0:1], jcol[:, 0:1], lows[:, r, 1:2], lows[:, r, 0:1], ALU.mult,
                                              ALU.add))
                link(dve.tensor_scalar(GE[:], LG[:], cnt[:, r, 0:1], None, ALU.is_ge, ALU.add, accum_out=cnt[:, r, 1:2]))
                dve.tensor_scalar(cnt[:, r, 2:3], cnt[:, r, 1:2], float(CAP), None, ALU.is_ge).then_inc(s_ind, 1)
                dve.wait_ge(s_m16, r + 1)
                link(dve.tensor_scalar(cnt[:, r, 3:4], psS[:, 300 + r:301 + r], -1.0, None, ALU.add))
                link(dve.tensor_scalar(lows[:, r + 1, 1:2], lows[:, r, 1:2], 1.0 / G16, None, ALU.mult))
                link(dve.scalar_tensor_tensor(lows[:, r + 1, 0:1], cnt[:, r, 3:4], lows[:, r, 1:2], lows[:, r, 0:1],
                                              ALU.mult, ALU.add))
            low_t, step = lows[:, ROUNDS, 0:1], lows[:, ROUNDS - 1, 1:2]
            link(dve.scalar_tensor_tensor(sel[:, 6:7], step, 2.0, low_t, ALU.mult, ALU.add))
            link(dve.tensor_scalar(GE[:], LG[:], sel[:, 6:7], None, ALU.is_ge, ALU.add, accum_out=sel[:, 7:8]))
            link(dve.scalar_tensor_tensor(CL[:], LG[:], low_t, GE[:], ALU.is_ge, ALU.subtract))
            link(dve.tensor_scalar(sel[:, 8:9], sel[:, 7:8], -1.0, float(CAP), ALU.mult, ALU.add))
            dve.wait_ge(s_exp, 1)
            link(dve.tensor_tensor_scan(LG[:], CL[:], CL[:], 0.0, ALU.bypass, ALU.add))
            link(dve.scalar_tensor_tensor(LG[:], LG[:], sel[:, 8:9], CL[:], ALU.is_le, ALU.mult))
            link(dve.tensor_tensor(LG[:], LG[:], GE[:], ALU.add))
            link(dve.reciprocal(sel[:, 9:10], sel[:, 2:3]))
            dve.scalar_tensor_tensor(EX[:], EX[:], sel[:, 9:10], LG[:], ALU.mult, ALU.mult).then_inc(s_w, 1)
            for g, (t0, t1) in enumerate(TG):
                dve.wait_ge(s_wT, g + 1)
                dve.tensor_copy(wtok[:, t0:t1, :],
                                O4[g][0:TP, 0:(t1 - t0) * P].rearrange("p (t e j) -> p t e j", e=NX, j=G16)[:, :, :, 0]
                                ).then_inc(s_wtok, 1)
            for t in range(T):
                dve.wait_ge(s_b2p, t + 1)
                dve.tensor_tensor(X1[:, t, :], X1[:, t, :], O4[t % 4][0:TP, :], ALU.add).then_inc(s_b2a, 1)
            dve.wait_ge(s_wtok, 3)
            dve.wait_ge(s_b2a, T)
            for e in range(NX):
                for t in range(T):
                    n = e * T + t
                    dve.wait_ge(s_mm2, n + 1)
                    if e >= 1:
                        dve.wait_ge(s_acc, n - T + 1)
                    dve.scalar_tensor_tensor(X1[:, t, :], O4[n % 4][0:TP, :], wtok[:, t, e:e + 1], X1[:, t, :],
                                             ALU.mult, ALU.add).then_inc(s_acc, 1)

        @block.tensor
        def _(pe):
            pe.wait_ge(s_diag, 1)
            pe.wait_ge(s_const, 1)
            pe.matmul(psS[0:TP, 0:TP], ones16[0:TP, 0:TP], diag16[:], start=True, stop=True).then_inc(s_rowps, 1)
            pe.wait_ge(s_gb, 16)
            pe.wait_ge(s_ident, 2)
            pe.wait_ge(s_rr, 1)
            pe.transpose(psS[:, 256:256 + KC], gb4[:], ident[0:KC, 0:KC]).then_inc(s_gbT, 1)

            for c in range(KC):
                if c >= 2:
                    pe.wait_ge(s_lo, c - 1)
                for o in range(KC):
                    pe.wait_ge(s_wscale, o + 1)
                    last = pe.transpose(TR[c % 2][:, o * P:(o + 1) * P], Wn[:, o, c * P:(c + 1) * P], ident[:])
                last.then_inc(s_tr, 1)
            pe.wait_ge(s_wscale, KC + 1)
            pe.wait_ge(s_const, 3)
            for k in range(2):
                for c in range(KC):
                    last = pe.matmul(H[k][0:TP, c * P:(c + 1) * P], ones[:, 0:TP], dscale[:, k, c, :], start=True, stop=True)
            last.then_inc(s_bc, 1)

            def turn(t):
                pe.wait_ge(s_xn, t + 1)
                pe.wait_ge(s_lo, KC + t - 1)
                for c in range(KC):
                    last = pe.transpose(TR[t % 2][:, c * TP:(c + 1) * TP], HB[:, t, c * P:(c + 1) * P],
                                        ident[0:TP, 0:TP])
                last.then_inc(s_tr, 1)

            def project(t):
                pe.wait_ge(s_lo, KC + t + 1)
                if t < 2:
                    pe.wait_ge(s_bcv, 2)
                else:
                    pe.wait_ge(s_hb, t - 1)
                for n, (a, w) in enumerate(((XNh, WTh), (XNl, WTh), (XNh, WTl))):
                    for c in range(KC):
                        last = pe.matmul(H[t % 2][0:TP, :], a[:, t % 2, c, :], w[:, c, :],
                                         start=(n == 0 and c == 0), stop=False)
                for k in range(2):
                    last = pe.matmul(H[t % 2][0:TP, :], onesr[:, 0:TP], brow[:, k, :], start=False, stop=(k == 1))
                last.then_inc(s_h, 1)

            turn(0)
            turn(1)
            pe.wait_ge(s_ek, 2)
            for k in range(2):
                for h in range(HC):
                    to = (k * HC + h) * (NW + 1)
                    last = pe.transpose(psS16[:, to:to + NW], ek16[:, k, h * P:(h + 1) * P], ident16[0:NW, 0:NW])
            last.then_inc(s_kps, 1)
            for t in range(T):
                project(t)
                if t + 2 < T:
                    turn(t + 2)

            pe.wait_ge(s_m, TP)
            pe.wait_ge(s_pad, 1)
            pe.wait_ge(s_hb, T)
            for b in range(NB):
                pe.wait_ge(s_n, b + 1)
                for k, (g0, g1) in enumerate(SETS):
                    if b:
                        pe.wait_ge(s_at, 2 * b - 1 + k)
                    for g in range(g0, g1):
                        for w in range(GW):
                            for h in range(HC):
                                i = (g * GW + w) * HC + h
                                last = pe.matmul(AB[k][:, g - g0, w * NK:(w + 1) * NK], OHM[:, :, b * CB + i],
                                                 OHN[:, b % 2, :, i], start=(h == 0), stop=(h == HC - 1))
                    last.then_inc(s_set, 1)

            pe.wait_ge(s_tot, 1)
            pe.matmul(psS[0:1, 0:1], tot[:, 0:1], ones[0:TP, 0:1], start=True, stop=True).then_inc(s_totps, 1)
            pe.wait_ge(s_flag, 1)
            general = pe.value_load(flag[0:1, 0:1], min_val=0, max_val=1)
            with pe.If(general):
                DC = N // 5
                pe.matmul(psS[0:1, 0:1], tot[:, 0:1], ones[0:TP, 0:1], start=True, stop=True).then_inc(s_gmm, 1)
                with pe.Fori(0, T) as q:
                    with pe.Fori(0, 5) as d:
                        group = q * 5 + d
                        pe.wait_ge(s_gev, group + 1)
                        pe.wait_ge(s_goh, group * (ROW // 2) + 1)
                        pe.matmul(psS[0:TP, 0:DC], ohs[:, 0, 0:TP], ohd[:, 0, :], start=True, stop=False,
                                  skip_group_check=True)
                        pe.matmul(psS[0:TP, 0:DC], ohs[:, 1, 0:TP], ohd[:, 1, :], start=False, stop=False,
                                  skip_group_check=True).then_inc(s_gmm, 1)
                        with pe.Fori(1, ROW // 2) as c:
                            pe.wait_ge(s_goh, group * (ROW // 2) + c + 1)
                            pe.matmul(psS[0:TP, 0:DC], ohs[:, 0, 0:TP], ohd[:, 0, :], start=False, stop=False,
                                      skip_group_check=True)
                            pe.matmul(psS[0:TP, 0:DC], ohs[:, 1, 0:TP], ohd[:, 1, :], start=False, stop=False,
                                      skip_group_check=True).then_inc(s_gmm, 1)
            pe.wait_ge(s_counts, 1)
            pe.wait_ge(s_b1, 16)
            pe.transpose(psS[:, 256:256 + NX * FC], b1row[:], ident[0:NX * FC, 0:NX * FC]).then_inc(s_b1T, 1)

            def aggregate(t):
                if t >= 2:
                    pe.wait_ge(s_res, t - 1)
                cols = slice(t * TP, (t + 1) * TP)
                for q in range(T):
                    for n, part in enumerate((HDh, HDl)):
                        if t == 0:
                            pe.wait_ge((s_hdh, s_hdl)[n], q + 1)
                        if q == T - 1 and n == 1:
                            with pe.If(general):
                                for q2 in range(T):
                                    for part2 in (HDh, HDl):
                                        pe.matmul(H[t % 2][0:TP, :], AT2[0:TP, q2, cols], part2[:, q2, :], start=False,
                                                  stop=False, skip_group_check=True)
                        last = pe.matmul(H[t % 2][0:TP, :], AT[0:TP, q, cols], part[:, q, :],
                                         start=(q == 0 and n == 0), stop=(q == T - 1 and n == 1))
                last.then_inc(s_agg, 1)

            def turn2(t):
                pe.wait_ge(s_xn2, t + 1)
                if t >= 2:
                    pe.wait_ge(s_lo2, t - 1)
                for c in range(KC):
                    last = pe.transpose(TR[t % 2][:, c * TP:(c + 1) * TP], xn2[:, t % 2, c * P:(c + 1) * P],
                                        ident[0:TP, 0:TP])
                last.then_inc(s_tr2, 1)

            def logits(g):
                t0, t1 = TG[g]
                pe.wait_ge(s_lo2, t1)
                pe.wait_ge(s_wrs, 1)
                cols = slice(t0 * TP, t1 * TP)
                for n, (w, a) in enumerate(((Wrh, XTh), (Wrl, XTh), (Wrh, XTl))):
                    for c in range(KC):
                        last = pe.matmul(psX[:, g, 0:(t1 - t0) * TP], w[:, c, :, :].rearrange("p e j -> p (e j)"),
                                         a[:, c, cols], start=(n == 0 and c == 0), stop=(n == 2 and c == KC - 1))
                last.then_inc(s_lgp, 1)

            aggregate(0)
            for t in range(1, T):
                aggregate(t)
                turn2(t - 1)
                if t == 6:
                    logits(0)
            turn2(T - 1)
            logits(1)
            logits(2)

            def hidden_layer(e, rounds):
                pe.wait_ge(s_w1l, e + 1)
                for i, (f, a, b) in enumerate(PIECES):
                    n = e * NP + i
                    if n >= 3:
                        pe.wait_ge(s_gelu, n - 2)
                    elif n == 0:
                        pe.wait_ge(s_lg, len(TG))
                    for k, (w, z) in enumerate(((W1h, XTh), (W1l, XTh), (W1h, XTl))):
                        for c in range(KC):
                            last = pe.matmul(psX[:, i % 3, 0:b - a], w[e % 2][:, c, f * P:(f + 1) * P],
                                             z[:, c, a:b], start=(k == 0 and c == 0), stop=(k == 2 and c == KC - 1))
                    last.then_inc(s_mm1, 1)
                    if i < len(rounds):
                        r = rounds[i]
                        pe.wait_ge(s_ind, r + 1)
                        pe.matmul(psS[:, 300 + r:301 + r], blk[:], cnt[:, r, 2:3], start=True, stop=True
                                  ).then_inc(s_m16, 1)

            def output_layer(e):
                pe.wait_ge(s_w2l, e + 1)
                pe.wait_ge(s_hl, NP * (e + 1))
                for t in range(T):
                    n = e * T + t
                    if n >= 4:
                        pe.wait_ge(s_acc, n - 3)
                    for k, (z, w) in enumerate(((Hh, W2h), (Hl, W2h), (Hh, W2l))):
                        for f in range(FC):
                            last = pe.matmul(O4[n % 4][0:TP, :], z[:, e % 2, f, t * TP:(t + 1) * TP],
                                             w[e % 2][:, f, :], start=(k == 0 and f == 0), stop=(k == 2 and f == FC - 1))
                    last.then_inc(s_mm2, 1)

            pe.wait_ge(s_blk, 4)
            hidden_layer(0, range(0, 4))
            hidden_layer(1, range(4, ROUNDS))
            pe.wait_ge(s_w, 1)
            for g, (t0, t1) in enumerate(TG):
                for t in range(t0, t1):
                    last = pe.transpose(O4[g][0:TP, (t - t0) * P:(t - t0 + 1) * P], EX[:, t * TP:(t + 1) * TP], ident[:])
                last.then_inc(s_wT, 1)
            pe.wait_ge(s_b2, 16)
            pe.wait_ge(s_wtok, 3)
            for t in range(T):
                if t >= 4:
                    pe.wait_ge(s_b2a, t - 3)
                pe.matmul(O4[t % 4][0:TP, :], EX[:, t * TP:(t + 1) * TP], b2z[:], start=True, stop=True).then_inc(s_b2p, 1)
            pe.wait_ge(s_b2a, T)
            for e in range(NX):
                output_layer(e)
                if e + 2 < NX:
                    hidden_layer(e + 2, ())


_INS = ['x', 'src', 'dst', 'L0_gnn_W', 'L0_gnn_b', 'L0_ffn_Wr', 'L0_ffn_W1', 'L0_ffn_b1', 'L0_ffn_W2', 'L0_ffn_b2']


def kernel(**inputs):
    import concourse.bacc as _bacc
    from concourse.bass_utils import run_bass_kernel_spmd as _run

    nc = _bacc.Bacc("TRN2", target_bir_lowering=False, num_devices=1)
    arrays, args = {}, []
    for name in _INS:
        a = np.ascontiguousarray(inputs[name])
        arrays[f"in_{name}"] = a
        args.append(nc.dram_tensor(f"in_{name}", a.shape, mybir.dt.from_np(a.dtype), kind="ExternalInput").ap())
    args.append(nc.dram_tensor("out", inputs["x"].shape, F32, kind="ExternalOutput").ap())
    gnn_ffn(nc, *args)
    return _run(nc, [arrays], core_ids=[0]).results[0]["out"]
```

```python
from contextlib import ExitStack

import numpy as np

import concourse.bass as bass
from concourse import mybir

ALU = mybir.AluOpType
ACT = mybir.ActivationFunctionType
AX = mybir.AxisListType
F32 = mybir.dt.float32
F32R = mybir.dt.float32r
F16 = mybir.dt.float16
I32 = mybir.dt.int32

P = 128
EPS = 1e-5
ROUND = 12582912.0


def gnn_ffn(nc, x, src, dst, gnn_W, gnn_b, Wr, W1, b1, W2, b2, out):
    N, D = x.shape
    E = src.shape[0]
    NX, _, F = W1.shape
    KC = D // P
    FC = F // P
    TP = 125
    T = N // TP
    CAP = min(512, N)
    ROW = E // TP

    WIN = 10
    NW = N // WIN
    HC = 3
    SLOT = HC * P
    NCH = NW * HC
    NB = 5
    WB = NW // NB
    CB = WB * HC
    GW = 5
    KEYS = WIN + 2
    NK = T * WIN
    SETS = [(0, 3), (3, 5)]
    NROOM = 272
    NPARTS = [(0, 2 * CB), (2 * CB, NROOM), (NROOM, NCH)]
    HSCALE = 16384.0
    G16 = 16
    ROUNDS = 7
    SPLIT = [(0, 120), (120, TP)]
    NU = 5
    TG = [(0, 4), (4, 8), (8, 10)]
    assert T * TP == N and TP * ROW == E and NX * G16 == P and NW <= P and NB * WB == NW

    with ExitStack() as ctx:
        def sb(name, shape, dt):
            return ctx.enter_context(nc.sbuf_tensor(name, shape, dt))

        def sem(name):
            return ctx.enter_context(nc.semaphore(name))

        ident = sb("ident", [P, P], F32)
        ident16 = sb("ident16", [P, P], F16)
        ones = sb("ones", [P, P], F32)
        ones16 = sb("ones16", [P, P], F16)
        blk = sb("blk", [P, P], F32)
        win0 = sb("win0", [P, 1], F32)
        rowid = sb("rowid", [P, 1], F32)
        jm = sb("jm", [P, 4], F32)
        jcol = sb("jcol", [P, 3], F32)
        dst_e = sb("dst_e", [TP, ROW], I32)
        src_e = sb("src_e", [TP, ROW], I32)
        diag16 = sb("diag16", [TP, TP], F16)
        sm = sb("sm", [P, 16], F32)
        smi = sb("smi", [P, 4], I32)
        junk = sb("junk", [P, 1], F32)
        keyM = sb("keyM", [P, NCH + 1], F16)
        keyN = sb("keyN", [P, NCH + 1], F16)
        bn = sb("bn", [TP, T, 6], F32)
        mv = sb("mv", [TP, T, 2], F32)
        rstd = sb("rstd", [TP, 3, T], F32)
        nmr = sb("nmr", [TP, T], F32)
        wsc = sb("wsc", [P, 8, KC], F32)
        gb4 = sb("gb4", [KC, P], F32)
        degp = sb("degp", [TP, T, NB * 2], F32)
        dis = sb("dis", [TP, 4, T], F32)
        tot = sb("tot", [TP, 2], F32)
        flag = sb("flag", [1, 2], I32)
        bn2 = sb("bn2", [TP, 2, 6], F32)
        mv2 = sb("mv2", [TP, T, 2], F32)
        rs2 = sb("rs2", [TP, 4, T], F32)
        b1row = sb("b1row", [NX * FC, P], F32)
        b1col = sb("b1col", [P, NX * FC], F32)
        mx = sb("mx", [P, 8], F32)
        sel = sb("sel", [P, 16], F32)
        cnt = sb("cnt", [P, ROUNDS, 4], F32)
        lows = sb("lows", [P, ROUNDS + 1, 2], F32)
        wtok = sb("wtok", [TP, T, NX], F32)
        inv_bc = sb("inv_bc", [TP, D], F32)
        onesr = sb("onesr", [1, P], F32R)
        brow = sb("brow", [1, 2, D], F32R)

        base = (nc.sbuf_base + 63) // 64 * 64
        plan = {}

        def at(name, shape, dt, off):
            size = int(np.prod(shape[1:])) * (2 if dt == F16 else 4)
            plan[name] = (off, off + size)
            return nc.alloc_sbuf_tensor_at(name, shape, dt, offset=base + off)

        def end(name):
            return (plan[name][1] + 63) // 64 * 64

        AT = at("AT", [P, T, N + 6], F16, 0)
        XNh = at("XNh", [P, 2, KC, TP], F32R, 0)
        XNl = at("XNl", [P, 2, KC, TP], F32R, end("XNh"))
        WTh = at("WTh", [P, KC, D], F32R, end("XNl"))
        WTl = at("WTl", [P, KC, D], F32R, end("WTh"))
        assert end("WTl") <= end("AT")
        HB = at("HB", [TP, T, D], F32, end("AT"))
        OHM = at("OHM", [P, P, NCH], F16, end("HB"))
        OHN = at("OHN", [P, NK, NROOM], F16, end("OHM"))
        room = nc.sbuf_usable_end - base
        Wn = at("Wn", [P, KC, D], F32, plan["OHN"][0])
        Wsq = at("Wsq", [P, D], F32, end("Wn"))
        grow = at("grow", [TP, ROW], I32, end("Wsq"))
        grow16 = at("grow16", [TP, ROW], F16, end("grow"))
        gd = at("gd", [NW, SLOT], I32, end("grow16"))
        gs = at("gs", [NW, SLOT], I32, end("gd"))
        ek = at("ek", [NW, 4, SLOT], F32, end("gs"))
        ek16 = at("ek16", [NW, 2, SLOT], F16, end("ek"))
        dscale = at("dscale", [P, 2, KC, P], F32, end("ek16"))
        cmp16 = at("cmp16", [TP, ROW], F16, end("dscale"))
        assert end("cmp16") <= end("OHN")
        HDh = at("HDh", [TP, T, D], F16, plan["OHN"][0])
        HDl = at("HDl", [TP, T, D], F16, end("HDh"))
        AT2 = at("AT2", [P, T, N + 6], F16, end("HDl"))
        dst_f = at("dst_f", [TP, ROW], F32, plan["OHM"][0])
        src_f = at("src_f", [TP, ROW], F32, end("dst_f"))
        srcq_f = at("srcq_f", [TP, ROW], F32, end("src_f"))
        iota_n = at("iota_n", [TP, N], F32, end("srcq_f"))
        ohs = at("ohs", [TP, 2, P], F16, end("iota_n"))
        ohd = at("ohd", [TP, 2, N // 5], F16, end("ohs"))
        atp = at("atp", [TP, N // 5], F32, end("ohd"))
        assert end("AT2") <= room
        X1 = at("X1", [TP, T, D], F32, plan["OHM"][0])
        XTh = at("XTh", [P, KC, N], F32R, end("X1"))
        XTl = at("XTl", [P, KC, N], F32R, end("XTh"))
        xn2 = at("xn2", [TP, 2, D], F32, end("XTl"))
        WrN = at("WrN", [P, KC, NX], F32, end("xn2"))
        Wrh = at("Wrh", [P, KC, NX, G16], F32R, end("WrN"))
        Wrl = at("Wrl", [P, KC, NX, G16], F32R, end("Wrh"))
        LG = at("LG", [P, N], F32, end("Wrl"))
        b2z = at("b2z", [P, D], F32, end("LG"))
        W1n = at("W1n", [P, 2, KC, F], F32, end("b2z"))
        W2n = at("W2n", [P, 2, FC, D], F32, end("W1n"))
        assert end("W2n") <= plan["OHN"][0], (end("W2n"), plan["OHN"][0])
        W1h, W1l, W2h, W2l = [], [], [], []
        for n, off in enumerate((plan["HB"][0], plan["OHN"][0])):
            W1h.append(at(f"W1h{n}", [P, KC, F], F32R, off))
            W1l.append(at(f"W1l{n}", [P, KC, F], F32R, end(f"W1h{n}")))
            W2h.append(at(f"W2h{n}", [P, FC, D], F32R, end(f"W1l{n}")))
            W2l.append(at(f"W2l{n}", [P, FC, D], F32R, end(f"W2h{n}")))
        Hh = at("Hh", [P, 2, FC, N], F32R, 0)
        HG = at("HG", [P, 2, 512], F32, end("W2l0"))
        assert end("Hh") <= plan["HB"][0] and end("HG") <= plan["OHM"][0]
        Hl = at("Hl", [P, 2, FC, N], F32R, end("W2l1"))
        EX = at("EX", [P, N], F32, end("Hl"))
        GE = at("GE", [P, N], F16, end("EX"))
        U = at("U", [TP, NU, D], F32, end("GE"))
        assert end("U") <= room, (end("U"), room)
        CL = at("CL", [P, N], F16, end("Hh"))
        EXh = at("EXh", [P, N], F32R, end("Hh"))
        assert end("EXh") <= plan["HB"][0]
        EXm = at("EXm", [P, N], F32R, plan["LG"][0])
        b2h = at("b2h", [P, D], F32R, plan["xn2"][0])
        b2m = at("b2m", [P, D], F32R, end("b2h"))
        assert end("b2m") <= end("xn2")

        banks = [ctx.enter_context(nc.psum_tensor(f"bank{i}", [P, 512], F32)) for i in range(3)]
        TR = banks[0:2]
        psX = ctx.enter_context(nc.psum_tensor("psX", [P, 3, 512], F32))
        psY = ctx.enter_context(nc.psum_tensor("psY", [P, 2, 512], F32))
        H = [banks[2], psY[:, 0, :]]
        O4 = [banks[0], banks[1], banks[2], psY[:, 0, :]]
        psB = psY[0:TP, 1, :]
        psS = psY[:, 1, :]
        LP = [psX[:, 2, :], psY[:, 0, :], banks[2]]
        psS16 = psS.bitcast(F16)
        AB = [psX, psY]

        s_dst = sem("s_dst")
        s_x = [sem(f"s_x{i}") for i in range(5)]
        s_W = sem("s_W")
        s_gb = sem("s_gb")
        s_ident = sem("s_ident")
        s_const = sem("s_const")
        s_link = sem("s_link")
        s_diag = sem("s_diag")
        s_rowps = sem("s_rowps")
        s_rr = sem("s_rr")
        s_grow = sem("s_grow")
        s_start = sem("s_start")
        s_gath = sem("s_gath")
        s_ek = sem("s_ek")
        s_kps = sem("s_kps")
        s_kps_read = sem("s_kps_read")
        s_key = sem("s_key")
        s_ssq = sem("s_ssq")
        s_gbT = sem("s_gbT")
        s_babs = sem("s_babs")
        s_wroot = sem("s_wroot")
        s_wscale = sem("s_wscale")
        s_var = sem("s_var")
        s_std = sem("s_std")
        s_nmr = sem("s_nmr")
        s_xn = sem("s_xn")
        s_tr = sem("s_tr")
        s_hi = sem("s_hi")
        s_lo = sem("s_lo")
        s_bc = sem("s_bc")
        s_bcv = sem("s_bcv")
        s_h = sem("s_h")
        s_hb = sem("s_hb")
        s_pad = sem("s_pad")
        s_blk = sem("s_blk")
        s_m = sem("s_m")
        s_n = sem("s_n")
        s_set = sem("s_set")
        s_at = sem("s_at")
        s_at2 = sem("s_at2")
        s_own = sem("s_own")
        s_src = sem("s_src")
        s_gsrc = sem("s_gsrc")
        s_gp = sem("s_gp")
        s_gend = sem("s_gend")
        s_tot = sem("s_tot")
        s_totps = sem("s_totps")
        s_flag = sem("s_flag")
        s_giota = sem("s_giota")
        s_goh = sem("s_goh")
        s_gmm = sem("s_gmm")
        s_gev = sem("s_gev")
        s_counts = sem("s_counts")
        s_droot = sem("s_droot")
        s_dis = sem("s_dis")
        s_hdh = sem("s_hdh")
        s_hdl = sem("s_hdl")
        s_x1 = [sem(f"s_x1{i}") for i in range(5)]
        s_agg = sem("s_agg")
        s_res = sem("s_res")
        s_var2 = sem("s_var2")
        s_std2 = sem("s_std2")
        s_nmr2 = sem("s_nmr2")
        s_xn2 = sem("s_xn2")
        s_tr2 = sem("s_tr2")
        s_hi2 = sem("s_hi2")
        s_lo2 = sem("s_lo2")
        s_Wr = sem("s_Wr")
        s_b1 = sem("s_b1")
        s_b2 = sem("s_b2")
        s_b2z = sem("s_b2z")
        s_b1T = sem("s_b1T")
        s_b1c = sem("s_b1c")
        s_wrs = sem("s_wrs")
        s_lgp = sem("s_lgp")
        s_lg = sem("s_lg")
        s_max = sem("s_max")
        s_exp = sem("s_exp")
        s_ind = sem("s_ind")
        s_m16 = sem("s_m16")
        s_w = sem("s_w")
        s_wT = sem("s_wT")
        s_wtok = sem("s_wtok")
        s_b2p = sem("s_b2p")
        s_b2a = sem("s_b2a")
        s_b2h = sem("s_b2h")
        s_b2m = sem("s_b2m")
        s_exm = sem("s_exm")
        s_exh = sem("s_exh")
        s_wx = sem("s_wx")
        s_u = sem("s_u")
        s_jm = sem("s_jm")
        s_w1n = [sem("s_w1n0"), sem("s_w1n1")]
        s_w2n = [sem("s_w2n0"), sem("s_w2n1")]
        s_w1h = sem("s_w1h")
        s_w2h = sem("s_w2h")
        s_w1l = sem("s_w1l")
        s_w2l = sem("s_w2l")
        s_mm1 = sem("s_mm1")
        s_gelu = sem("s_gelu")
        s_hh = sem("s_hh")
        s_hl = sem("s_hl")
        s_mm2 = sem("s_mm2")
        s_acc = sem("s_acc")
        s_out = sem("s_out")
        sets = len(SETS)
        OUT = [(0, 2), (2, 4), (4, 6), (6, 8), (8, 9), (9, 10)]
        PIECES = [(f, a, b) for a, b in ((0, 500), (500, 1000), (1000, N)) for f in range(FC)]
        TURNS = {2: {5: 0, 11: 1}, 5: {2: 2}, 6: {5: 3}, 7: {7: 4}, 8: {4: 5}, 9: {3: 6}}
        NP = len(PIECES)

        x_v = x.rearrange("(t p) d -> p t d", p=TP)
        out_v = out.rearrange("(t p) d -> p t d", p=TP)
        dst_v = dst.rearrange("(r c) -> r c", c=ROW)
        src_v = src.rearrange("(r c) -> r c", c=ROW)

        block = ctx.enter_context(nc.Block())

        @block.sync
        def _(sp):
            for a, b in SPLIT:
                sp.dma_start(dst_e[a:b, :], dst_v[a:b, :]).then_inc(s_dst, 16)
            for i in range(5):
                if i == 1:
                    sp.wait_ge(s_grow, 16)
                for a, b in SPLIT:
                    sp.dma_start(HB[a:b, 2 * i:2 * i + 2, :], x_v[a:b, 2 * i:2 * i + 2, :]).then_inc(s_x[i], 16)

            for a, b in SPLIT:
                sp.dma_start(src_e[a:b, :], src_v[a:b, :]).then_inc(s_src, 16)
            sp.dma_start(b1row[:], b1.rearrange("e (f p) -> (e f) p", p=P)).then_inc(s_b1, 16)
            sp.wait_ge(s_counts, 1)
            for i in range(5):
                for a, b in SPLIT:
                    sp.dma_start(X1[a:b, 2 * i:2 * i + 2, :], x_v[a:b, 2 * i:2 * i + 2, :]).then_inc(s_x1[i], 16)
                if i == 0:
                    sp.dma_start(WrN[:], Wr.rearrange("(c p) e -> p c e", p=P)).then_inc(s_Wr, 16)
            for e in range(NX):
                if e >= 2:
                    sp.wait_ge(s_w1l, e - 1)
                    sp.wait_ge(s_w1h, e - 1)
                sp.dma_start(W1n[:, e % 2, :, :], W1[e].rearrange("(c p) f -> p c f", p=P)).then_inc(s_w1n[e % 2], 16)
                if e >= 2:
                    sp.wait_ge(s_w2l, e - 1)
                    sp.wait_ge(s_w2h, e - 1)
                sp.dma_start(W2n[:, e % 2, :, :], W2[e].rearrange("(c p) d -> p c d", p=P)).then_inc(s_w2n[e % 2], 16)
                if e == 0:
                    sp.wait_ge(s_b2z, 1)
                    for j in range(3):
                        sp.dma_start(b2z[j:P:G16, :], b2).then_inc(s_b2, 16)
            for t0, t1 in OUT:
                sp.wait_ge(s_acc, (NX - 1) * T + t1)
                for a, b in SPLIT:
                    sp.dma_start(out_v[a:b, t0:t1, :], X1[a:b, t0:t1, :]).then_inc(s_out, 16)
            sp.wait_ge(s_out, 16 * 2 * len(OUT))
            sp.wait_ge(s_src, 32)

        @block.gpsimd
        def _(pool):
            pool.memset(ident[:], 0.0).then_inc(s_ident, 1)
            pool.memset(ones16[:], 1.0).then_inc(s_const, 1)
            pool.wait_ge(s_ident, 1)
            pool.affine_select(out=ident[:], in_=ident[:], compare_op=ALU.not_equal, fill=1.0, base=0,
                               pattern=[[-1, P]], channel_multiplier=1).then_inc(s_ident, 1)
            pool.iota(win0[:], pattern=[[0, 1]], base=0, channel_multiplier=WIN,
                      allow_small_or_imprecise_dtypes=True).then_inc(s_const, 1)
            pool.memset(ones[:], 1.0).then_inc(s_const, 1)
            pool.memset(OHM[:, TP:P, :].rearrange("p a c -> p (a c)"), 0.0).then_inc(s_pad, 1)
            pool.wait_ge(s_rr, 1)
            pool.indirect_dma_start(out=grow[:], out_offset=None, in_=dst_v,
                                    in_offset=bass.IndirectOffsetOnAxis(ap=smi[0:TP, 0:1], axis=0)
                                    ).then_inc(s_grow, 16)
            pool.wait_ge(s_start, 1)
            for lst, to in ((dst, gd), (src, gs)):
                pool.indirect_dma_start(out=to[:], out_offset=None, in_=lst.rearrange("(a n) -> a n", a=1),
                                        in_offset=bass.IndirectOffsetOnAxis(ap=smi[0:NW, 1:2], axis=1)
                                        ).then_inc(s_gath, 16)

            pool.memset(blk[:], 1.0).then_inc(s_blk, 1)
            pool.iota(rowid[:], pattern=[[0, 1]], base=0, channel_multiplier=1,
                      allow_small_or_imprecise_dtypes=True).then_inc(s_blk, 1)
            blk_v = blk[:].rearrange("p (g j) -> p g j", j=G16)
            pool.wait_ge(s_blk, 2)
            pool.affine_select(out=blk_v, in_=blk_v, compare_op=ALU.is_ge, fill=0.0, base=0,
                               pattern=[[-G16, NX], [0, G16]], channel_multiplier=1).then_inc(s_blk, 1)
            pool.wait_ge(s_blk, 3)
            pool.affine_select(out=blk_v, in_=blk_v, compare_op=ALU.is_ge, fill=0.0, base=G16 - 1,
                               pattern=[[G16, NX], [0, G16]], channel_multiplier=-1).then_inc(s_blk, 1)

            for b in range(NB):
                pool.wait_ge(s_at, min(2 * b + 2, 2 * NB - 1))
                if b == NB - 1:
                    pool.wait_ge(s_at2, 1)
                for t in (2 * b, 2 * b + 1):
                    own = AT[0:TP, t, t * TP:(t + 1) * TP]
                    pool.tensor_tensor(own, own, ident16[0:TP, 0:TP], ALU.add).then_inc(s_own, 1)

            pool.wait_ge(s_flag, 1)
            general = pool.value_load(flag[0:1, 0:1], min_val=0, max_val=1)
            with pool.If(general):
                pool.iota(iota_n[:], pattern=[[1, N]], base=0, channel_multiplier=0,
                          allow_small_or_imprecise_dtypes=True).then_inc(s_giota, 1)

            pool.wait_ge(s_counts, 1)
            pool.memset(b2z[:], 0.0).then_inc(s_b2z, 1)

            def low(to, full, high, done):
                pool.tensor_tensor(to, full, high.bitcast(F32), ALU.subtract).then_inc(done, 1)

            def low_w1(e):
                if e >= 2:
                    pool.wait_ge(s_mm1, NP * (e - 1))
                pool.wait_ge(s_w1h, e + 1)
                pool.wait_ge(s_w1n[e % 2], 16 * (e // 2 + 1))
                low(W1l[e % 2][:], W1n[:, e % 2, :, :], W1h[e % 2][:], s_w1l)

            def low_w2(e):
                if e >= 2:
                    pool.wait_ge(s_mm2, T * (e - 1))
                pool.wait_ge(s_w2h, e + 1)
                pool.wait_ge(s_w2n[e % 2], 16 * (e // 2 + 1))
                low(W2l[e % 2][:], W2n[:, e % 2, :, :], W2h[e % 2][:], s_w2l)

            low_w1(0)
            low_w2(0)
            low_w1(1)
            for e in range(NX):
                for i, (f, a, b) in enumerate(PIECES):
                    pool.wait_ge(s_hh, e * NP + i + 1)
                    if e >= 2:
                        pool.wait_ge(s_mm2, T * (e - 1))
                    low(Hl[:, e % 2, f, a:b], HG[:, i % 2, 0:b - a], Hh[:, e % 2, f, a:b], s_hl)
                if e + 1 < NX:
                    low_w2(e + 1)
                if e + 2 < NX:
                    low_w1(e + 2)

        @block.scalar
        def _(act):
            act.dma_start(Wn[:], gnn_W.rearrange("(c p) i -> p c i", p=P)).then_inc(s_W, 16)
            act.dma_start(gb4[:], gnn_b.rearrange("(c p) -> c p", p=P)).then_inc(s_gb, 16)
            act.wait_ge(s_W, 16)
            for c in range(KC):
                if c:
                    act.wait_ge(s_ssq, c)
                act.activation(Wsq[:], Wn[:, c, :], ACT.Square, accum_out=wsc[:, 0, c:c + 1]).then_inc(s_ssq, 1)
            act.wait_ge(s_ssq, KC)
            act.activation(wsc[:, 1, :], wsc[:, 0, :], ACT.Sqrt, scale=float(D)).then_inc(s_wroot, 1)

            def root(g):
                act.wait_ge(s_var, g + 1)
                act.activation(rstd[:, 1, 2 * g:2 * g + 2], rstd[:, 0, 2 * g:2 * g + 2], ACT.Sqrt).then_inc(s_std, 1)

            def norm(t):
                act.wait_ge(s_nmr, t // 2 + 1)
                act.activation(HB[:, t, :], HB[:, t, :], ACT.Identity, bias=nmr[:, t:t + 1],
                               scale=rstd[:, 2, t:t + 1]).then_inc(s_xn, 1)

            def high_w(c):
                act.wait_ge(s_tr, c + 1)
                act.activation(WTh[:, c, :], TR[c % 2][:], ACT.Copy).then_inc(s_hi, 1)

            def high_x(t):
                act.wait_ge(s_tr, KC + t + 1)
                if t >= 2:
                    act.wait_ge(s_h, t - 1)
                act.activation(XNh[:, t % 2, :, :].rearrange("p a c -> p (a c)"), TR[t % 2][:, 0:KC * TP],
                               ACT.Copy).then_inc(s_hi, 1)

            def hidden(t):
                act.wait_ge(s_h, t + 1)
                act.activation(HB[:, t, :], H[t % 2][0:TP, :], ACT.Copy).then_inc(s_hb, 1)

            root(0)
            high_w(0)
            high_w(1)
            norm(0)
            norm(1)
            high_w(2)
            high_w(3)
            root(1)
            for t in range(T):
                high_x(t)
                if t + 2 < T:
                    norm(t + 2)
                if t < 3:
                    root(t + 2)
                if t >= 1:
                    hidden(t - 1)
            hidden(T - 1)

            for b in range(NB):
                for k, (g0, g1) in enumerate(SETS):
                    if 2 * b + k == 2 * NB - 2:
                        continue
                    act.wait_ge(s_set, 2 * b + k + 1)
                    ps = AB[k][0:TP, :, 0:GW * NK].rearrange("p g (w q d) -> p q g w d", q=T, d=WIN)
                    d0 = (b * 5 + g0) * GW * WIN
                    for q in range(T):
                        to = AT[0:TP, q, d0:d0 + (g1 - g0) * GW * WIN].rearrange("p (g w d) -> p g w d", w=GW, d=WIN)
                        last = act.activation(to, ps[:, q], ACT.Copy, accum_out=degp[:, q, 2 * b + k:2 * b + k + 1])
                    last.then_inc(s_at, 1)

            act.wait_ge(s_counts, 1)
            act.activation(dis[:, 2, :], dis[:, 1, :], ACT.Sqrt).then_inc(s_droot, 1)
            act.wait_ge(s_dis, 1)
            for t in range(T):
                act.activation(HDh[:, t, :], HB[:, t, :], ACT.Copy, scale=dis[:, 3, t:t + 1]).then_inc(s_hdh, 1)

            def high_w1(e):
                if e >= 2:
                    act.wait_ge(s_mm1, NP * (e - 1))
                elif e == 0:
                    act.wait_ge(s_hdl, T)
                else:
                    act.wait_ge(s_agg, T)
                act.wait_ge(s_w1n[e % 2], 16 * (e // 2 + 1))
                act.activation(W1h[e % 2][:], W1n[:, e % 2, :, :], ACT.Copy).then_inc(s_w1h, 1)

            def high_w2(e):
                if e >= 2:
                    act.wait_ge(s_mm2, T * (e - 1))
                act.wait_ge(s_w2n[e % 2], 16 * (e // 2 + 1))
                act.activation(W2h[e % 2][:], W2n[:, e % 2, :, :], ACT.Copy).then_inc(s_w2h, 1)

            def root2(t):
                act.wait_ge(s_var2, t + 1)
                act.activation(rs2[:, 1, t:t + 1], rs2[:, 0, t:t + 1], ACT.Sqrt).then_inc(s_std2, 1)

            def norm2(t):
                act.wait_ge(s_nmr2, t + 1)
                if t >= 2:
                    act.wait_ge(s_tr2, t - 1)
                act.activation(xn2[:, t % 2, :], X1[:, t, :], ACT.Identity, bias=rs2[:, 3, t:t + 1],
                               scale=rs2[:, 2, t:t + 1]).then_inc(s_xn2, 1)

            def high_x2(t):
                act.wait_ge(s_tr2, t + 1)
                act.activation(XTh[:, :, t * TP:(t + 1) * TP],
                               TR[t % 2][:, 0:KC * TP].rearrange("p (c n) -> p c n", c=KC), ACT.Copy).then_inc(s_hi2, 1)

            for t in range(T):
                if t >= 2:
                    high_x2(t - 2)
                root2(t)
                norm2(t)
                if t == 4:
                    high_w1(0)
                if t == 5:
                    high_w2(0)
            high_x2(T - 2)
            high_x2(T - 1)
            for g, (t0, t1) in enumerate(TG):
                act.wait_ge(s_lgp, g + 1)
                act.activation(LG[:, t0 * TP:t1 * TP], LP[g][:, 0:(t1 - t0) * TP], ACT.Copy).then_inc(s_lg, 1)
            act.wait_ge(s_max, 1)
            act.activation(EX[:], LG[:], ACT.Exp, bias=sel[:, 1:2], accum_out=sel[:, 2:3]).then_inc(s_exp, 1)
            high_w1(1)
            act.wait_ge(s_b2, 48)
            act.wait_ge(s_tr2, T)
            act.wait_ge(s_jm, 1)
            act.activation(b2h[:], b2z[:], ACT.Copy).then_inc(s_b2h, 1)
            act.wait_ge(s_b2h, 1)
            act.activation(b2z[:], b2z[:], ACT.Copy, scale=jm[:, 2:3]).then_inc(s_b2h, 1)

            act.wait_ge(s_b1c, 1)
            for e in range(NX):
                for i, (f, a, b) in enumerate(PIECES):
                    n = e * NP + i
                    act.wait_ge(s_mm1, n + 1)
                    if n >= 2:
                        act.wait_ge(s_hl, n - 1)
                    if e >= 2:
                        act.wait_ge(s_mm2, T * (e - 1))
                    act.activation(HG[:, i % 2, 0:b - a], psX[:, i % 3, 0:b - a], ACT.Gelu,
                                   bias=b1col[:, e * FC + f:e * FC + f + 1]).then_inc(s_gelu, 1)
                    act.wait_ge(s_gelu, n + 1)
                    act.activation(Hh[:, e % 2, f, a:b], HG[:, i % 2, 0:b - a], ACT.Copy).then_inc(s_hh, 1)
                if e == 1:
                    for t in range(NU):
                        act.wait_ge(s_mm2, t + 1)
                        act.activation(U[:, t, :], O4[t % 4][0:TP, :], ACT.Copy).then_inc(s_u, 1)
                    act.wait_ge(s_w, 1)
                    act.activation(EXh[:], EX[:], ACT.Copy).then_inc(s_exh, 1)
                    act.activation(LG[:], EX[:], ACT.Copy, scale=jm[:, 0:1]).then_inc(s_exh, 1)
                if e + 1 < NX:
                    high_w2(e + 1)
                if e + 2 < NX:
                    high_w1(e + 2)

        @block.vector
        def _(dve):
            chain = [0]

            def link(ins):
                chain[0] += 1
                ins.then_inc(s_link, 1)
                dve.wait_ge(s_link, chain[0])

            dve.wait_ge(s_ident, 2)
            link(dve.tensor_copy(ident16[:], ident[:]))
            dve.wait_ge(s_dst, 32)
            dve.tensor_scalar(diag16[:], ident16[0:TP, 0:TP], dst_e[:, 0:1], None, ALU.mult).then_inc(s_diag, 1)

            def stats(t):
                dve.wait_ge(s_x[t // 2], 32)
                link(dve.bn_stats(bn[:, t, :], HB[:, t, :]))
                link(dve.bn_aggr(mv[:, t, :], bn[:, t, :]))

            def variances(g):
                a, b = 2 * g, 2 * g + 2
                dve.tensor_scalar(rstd[:, 0, a:b], mv[:, a:b, 1], EPS, None, ALU.add).then_inc(s_var, 1)

            def scales(g):
                a, b = 2 * g, 2 * g + 2
                dve.wait_ge(s_std, g + 1)
                link(dve.reciprocal(rstd[:, 2, a:b], rstd[:, 1, a:b]))
                dve.scalar_tensor_tensor(nmr[:, a:b], mv[:, a:b, 0], -1.0, rstd[:, 2, a:b], ALU.mult,
                                         ALU.mult).then_inc(s_nmr, 1)

            dve.wait_ge(s_rowps, 1)
            dve.wait_ge(s_const, 3)
            link(dve.tensor_scalar(cmp16[0:TP, 0:TP], psS[0:TP, 0:TP], win0[0:TP, :], None, ALU.is_lt, ALU.add,
                                   accum_out=sm[0:TP, 0:1]))
            link(dve.tensor_scalar(sm[0:TP, 1:2], sm[0:TP, 0:1], -1.0, 0.0, ALU.add, ALU.max))
            dve.tensor_copy(smi[0:TP, 0:1], sm[0:TP, 1:2]).then_inc(s_rr, 1)
            for t in range(2):
                stats(t)
            variances(0)
            dve.wait_ge(s_grow, 16)
            link(dve.tensor_copy(grow16[:], grow[:]))
            link(dve.tensor_scalar(cmp16[:], grow16[:], win0[0:TP, :], None, ALU.is_lt, ALU.add,
                                   accum_out=sm[0:TP, 2:3]))
            link(dve.scalar_tensor_tensor(sm[0:TP, 3:4], sm[0:TP, 1:2], float(ROW), sm[0:TP, 2:3], ALU.mult, ALU.add))
            link(dve.tensor_scalar(sm[0:TP, 4:5], sm[0:TP, 3:4], float(E - SLOT), None, ALU.min))
            dve.tensor_copy(smi[0:NW, 1:2], sm[0:NW, 4:5]).then_inc(s_start, 1)

            dve.wait_ge(s_gbT, 1)
            link(dve.tensor_scalar(wsc[:, 2, :], psS[:, 256:256 + KC], -1.0, None, ALU.mult))
            link(dve.tensor_tensor(wsc[:, 3, :], psS[:, 256:256 + KC], wsc[:, 2, :], ALU.max))
            dve.wait_ge(s_wroot, 1)
            link(dve.scalar_tensor_tensor(wsc[:, 4, :], wsc[:, 1, :], 1e-30, wsc[:, 3, :], ALU.add, ALU.add))
            link(dve.tensor_scalar(wsc[:, 5, :], wsc[:, 4, :], 1.0 / HSCALE, None, ALU.mult))
            link(dve.reciprocal(wsc[:, 6, :], wsc[:, 5, :]))
            link(dve.scalar_tensor_tensor(wsc[:, 7, :], wsc[:, 2, :], -1.0, wsc[:, 6, :], ALU.mult, ALU.mult))
            for c in range(KC):
                dve.tensor_scalar(Wn[:, c, :], Wn[:, c, :], wsc[:, 6, c:c + 1], None, ALU.mult).then_inc(s_wscale, 1)
            def pair(g):
                stats(2 * g)
                stats(2 * g + 1)
                variances(g)

            def low_w(c):
                dve.wait_ge(s_hi, c + 1)
                dve.tensor_tensor(WTl[:, c, :], TR[c % 2][:], WTh[:, c, :].bitcast(F32), ALU.subtract).then_inc(s_lo, 1)

            low_w(0)
            scales(0)
            low_w(1)
            pair(1)

            dve.wait_ge(s_gath, 32)
            link(dve.tensor_scalar(ek[:, 0, :], gd[:], win0[0:NW, :], None, ALU.subtract))
            link(dve.tensor_scalar(ek[:, 0, :], ek[:, 0, :], -1.0, float(WIN), ALU.max, ALU.min))
            link(dve.tensor_scalar(ek[:, 1, :], gs[:], 1.0 / TP, 0.5 / TP - 0.5, ALU.mult, ALU.add))
            link(dve.tensor_scalar(ek[:, 2, :], ek[:, 1, :], ROUND, -ROUND, ALU.add, ALU.add))
            dve.scalar_tensor_tensor(ek16[:, 0, :], ek[:, 2, :], -float(TP), gs[:], ALU.mult, ALU.add).then_inc(s_ek, 1)
            dve.scalar_tensor_tensor(ek16[:, 1, :], ek[:, 2, :], float(KEYS), ek[:, 0, :], ALU.mult,
                                     ALU.add).then_inc(s_ek, 1)

            def low_x(t):
                dve.wait_ge(s_hi, KC + t + 1)
                dve.tensor_tensor(XNl[:, t % 2, :, :].rearrange("p a c -> p (a c)"), TR[t % 2][:, 0:KC * TP],
                                  XNh[:, t % 2, :, :].rearrange("p a c -> p (a c)").bitcast(F32),
                                  ALU.subtract).then_inc(s_lo, 1)

            def bias_row():
                dve.tensor_copy(onesr[:], ones[0:1, :]).then_inc(s_bcv, 1)
                dve.wait_ge(s_bc, 1)
                link(dve.tensor_copy(brow[:, 0, :], psS[0:1, :]))
                dve.tensor_tensor(brow[:, 1, :], psS[0:1, :], brow[:, 0, :].bitcast(F32),
                                  ALU.subtract).then_inc(s_bcv, 1)

            def inverse_row():
                dve.wait_ge(s_bc, 2)
                dve.tensor_copy(inv_bc[:], psS[0:TP, :])

            low_w(2)
            low_w(3)
            dve.wait_ge(s_kps, 1)
            for k, to in ((0, keyM), (1, keyN)):
                last = dve.tensor_copy(to[:, 0:NCH].rearrange("p (w h) -> p h w", h=HC),
                                       psS16[:, k * HC * (NW + 1):(k + 1) * HC * (NW + 1)].rearrange(
                                           "p (h w) -> p h w", h=HC)[:, :, 0:NW])
            link(last)
            junk_col = dve.tensor_copy(junk[:, 0:1], win0[:])
            junk_col.then_inc(s_kps_read, 1)
            for c in range(KC):
                dve.tensor_scalar(dscale[:, 0, c, :], ident[:], wsc[:, 7, c:c + 1], None, ALU.mult)
                last = dve.tensor_scalar(dscale[:, 1, c, :], ident[:], wsc[:, 5, c:c + 1], None, ALU.mult)
            last.then_inc(s_wscale, 1)

            between = {1: (low_x, 0), 3: (scales, 1), 6: (pair, 2), 9: (bias_row,), 13: (low_x, 1), 18: (pair, 3),
                       24: (scales, 2), 26: (inverse_row,), 28: (pair, 4), 30: (scales, 3), 36: (low_x, 2),
                       40: (scales, 4), 54: (low_x, 3), 71: (low_x, 4), 88: (low_x, 5), 105: (low_x, 6),
                       122: (low_x, 7), TP + 26: (low_x, 8), TP + 53: (low_x, 9)}

            def aside(j):
                if j in between:
                    step, *which = between[j]
                    step(*which)

            for j in range(TP):
                dve.tensor_scalar(OHM[:, j, :], keyM[:, 0:NCH], float(j), None, ALU.is_equal).then_inc(s_m, 1)
                aside(j)
            for n0, n1 in NPARTS:
                if n0 == NROOM:
                    dve.wait_ge(s_set, 4)
                for n in range(NK):
                    key = float(n // WIN * KEYS + n % WIN)
                    last = dve.tensor_scalar(OHN[:, n, n0 % NROOM:(n1 - 1) % NROOM + 1], keyN[:, n0:n1], key, None,
                                             ALU.is_equal)
                    if n0 == 0:
                        aside(TP + n)
                last.then_inc(s_n, 1)

            dve.wait_ge(s_set, 2 * NB - 1)
            ps = psX[0:TP, :, 0:GW * NK].rearrange("p g (w q d) -> p q g w d", q=T, d=WIN)
            g0, g1 = SETS[0]
            d0 = (NB - 1) * 5 * GW * WIN
            for q in range(T):
                to = AT[0:TP, q, d0:d0 + (g1 - g0) * GW * WIN].rearrange("p (g w d) -> p g w d", w=GW, d=WIN)
                last = dve.tensor_scalar(to, ps[:, q], 1.0, None, ALU.mult, ALU.add,
                                         accum_out=degp[:, q, 2 * NB - 2:2 * NB - 1])
            last.then_inc(s_at2, 1)
            dve.wait_ge(s_at2, 1)
            dve.wait_ge(s_at, 2 * NB - 1)
            link(dve.tensor_reduce(dis[:, 0, :], degp[:], AX.X, ALU.add))
            dve.tensor_reduce(tot[:, 0:1], dis[:, 0, :], AX.X, ALU.add).then_inc(s_tot, 1)
            link(dve.tensor_scalar(dis[:, 1, :], dis[:, 0, :], 1.0, None, ALU.add))
            dve.wait_ge(s_totps, 1)
            dve.tensor_scalar(flag[:, 0:1], psS[0:1, 0:1], float(E), None, ALU.not_equal).then_inc(s_flag, 1)
            dve.wait_ge(s_flag, 1)
            general = dve.value_load(flag[0:1, 0:1], min_val=0, max_val=1)
            with dve.If(general):
                dve.wait_ge(s_src, 32)
                dve.wait_ge(s_giota, 1)
                dve.wait_ge(s_own, T)
                dve.tensor_copy(dst_f[:], dst_e[:]).then_inc(s_gev, 1)
                dve.tensor_copy(src_f[:], src_e[:]).then_inc(s_gsrc, 1)
                DC = N // 5
                with dve.Fori(0, T) as q:
                    dve.wait_ge(s_gsrc, q + 1)
                    dve.wait_ge(s_gmm, q * (5 * ROW // 2) + 1)
                    dve.tensor_scalar(srcq_f[:], src_f[:], iota_n[:, bass.ds(q * TP, 1)], None,
                                      ALU.subtract).then_inc(s_gsrc, 1)
                    dve.wait_ge(s_gsrc, q + 2)
                    dve.tensor_copy(junk[:, 0:1], win0[:])
                    with dve.Fori(0, 5) as d:
                        with dve.Fori(0, ROW // 2) as c:
                            step = (q * 5 + d) * (ROW // 2) + c
                            dve.wait_ge(s_gmm, step + 1)
                            for k in range(2):
                                dve.tensor_scalar(ohs[:, k, 0:TP], iota_n[:, 0:TP], srcq_f[:, bass.ds(c * 2 + k, 1)],
                                                  None, ALU.is_equal)
                                last = dve.tensor_scalar(ohd[:, k, :], iota_n[:, bass.ds(d * DC, DC)],
                                                         dst_f[:, bass.ds(c * 2 + k, 1)], None, ALU.is_equal)
                            last.then_inc(s_goh, 1)
                        group = q * 5 + d
                        dve.wait_ge(s_gmm, (group + 1) * (ROW // 2) + 1)
                        dve.tensor_copy(atp[:], psS[0:TP, 0:DC]).then_inc(s_gp, 1)
                        dve.wait_ge(s_gp, group * 2 + 1)
                        part = AT[0:TP, bass.ds(q, 1), bass.ds(d * DC, DC)].rearrange("p a n -> p (a n)")
                        part2 = AT2[0:TP, bass.ds(q, 1), bass.ds(d * DC, DC)].rearrange("p a n -> p (a n)")
                        dve.tensor_copy(part, atp[:]).then_inc(s_gp, 1)
                        dve.wait_ge(s_gp, group * 2 + 2)
                        dve.tensor_tensor(part2, atp[:], part, ALU.subtract).then_inc(s_gev, 1)
                dve.wait_ge(s_gev, 5 * T + 1)
                for t in range(T):
                    own = AT2[0:TP, t, t * TP:(t + 1) * TP]
                    last = dve.tensor_tensor(own, own, ident16[0:TP, 0:TP], ALU.add)
                last.then_inc(s_gend, 1)
                dve.wait_ge(s_gend, 1)
                dve.tensor_reduce(dis[:, 0, :], AT[0:TP, :, 0:N], AX.X, ALU.add)
                dve.tensor_reduce(dis[:, 2, :], AT2[0:TP, :, 0:N], AX.X, ALU.add).then_inc(s_gend, 1)
                dve.wait_ge(s_gend, 2)
                dve.tensor_tensor(dis[:, 1, :], dis[:, 0, :], dis[:, 2, :], ALU.add).then_inc(s_gend, 1)
                dve.wait_ge(s_gend, 3)
            dve.tensor_copy(junk[:, 0:1], win0[:]).then_inc(s_counts, 1)

            dve.wait_ge(s_droot, 1)
            dve.reciprocal(dis[:, 3, :], dis[:, 2, :]).then_inc(s_dis, 1)
            dve.wait_ge(s_dis, 1)
            for t in range(T):
                dve.wait_ge(s_hdh, t + 1)
                dve.scalar_tensor_tensor(HDl[:, t, :], HB[:, t, :], dis[:, 3, t:t + 1], HDh[:, t, :], ALU.mult,
                                         ALU.subtract).then_inc(s_hdl, 1)

            dve.wait_ge(s_Wr, 16)
            wide = WrN[:].unsqueeze(3).to_broadcast([P, KC, NX, G16])
            link(dve.tensor_copy(Wrh[:], wide))
            dve.tensor_tensor(Wrl[:], wide, Wrh[:].bitcast(F32), ALU.subtract).then_inc(s_wrs, 1)
            dve.wait_ge(s_blk, 2)
            link(dve.tensor_scalar(jcol[:, 1:2], rowid[:], 1.0 / G16, 0.5 / G16 - 0.5, ALU.mult, ALU.add))
            link(dve.tensor_scalar(jcol[:, 2:3], jcol[:, 1:2], ROUND, -ROUND, ALU.add, ALU.add))
            link(dve.scalar_tensor_tensor(jcol[:, 0:1], jcol[:, 2:3], -float(G16), rowid[:], ALU.mult, ALU.add))

            for j in range(2):
                link(dve.tensor_scalar(jm[:, 2 * j:2 * j + 1], jcol[:, 0:1], float(j + 1), None, ALU.is_equal))
                last = dve.tensor_scalar(jm[:, 2 * j + 1:2 * j + 2], jm[:, 2 * j:2 * j + 1], -2.0, 1.0, ALU.mult, ALU.add)
            last.then_inc(s_jm, 1)

            def low_x2(t):
                dve.wait_ge(s_hi2, t + 1)
                to = XTl[:, :, t * TP:(t + 1) * TP]
                dve.tensor_tensor(to, TR[t % 2][:, 0:KC * TP].rearrange("p (c n) -> p c n", c=KC),
                                  XTh[:, :, t * TP:(t + 1) * TP].bitcast(F32), ALU.subtract).then_inc(s_lo2, 1)

            for t in range(T):
                dve.wait_ge(s_agg, t + 1)
                dve.wait_ge(s_x1[t // 2], 32)
                if t >= 2:
                    dve.wait_ge(s_tr2, t - 1)
                tmp = xn2[:, t % 2, :]
                dve.scalar_tensor_tensor(tmp, H[t % 2][0:TP, :], 0.0, inv_bc[:], ALU.max, ALU.mult).then_inc(s_res, 1)
                dve.wait_ge(s_res, t + 1)
                link(dve.scalar_tensor_tensor(X1[:, t, :], tmp, dis[:, 3, t:t + 1], X1[:, t, :], ALU.mult, ALU.add))
                link(dve.bn_stats(bn2[:, t % 2, :], X1[:, t, :]))
                link(dve.bn_aggr(mv2[:, t, :], bn2[:, t % 2, :]))
                dve.tensor_scalar(rs2[:, 0, t:t + 1], mv2[:, t, 1:2], EPS, None, ALU.add).then_inc(s_var2, 1)
                if t >= 2:
                    low_x2(t - 2)
                dve.wait_ge(s_std2, t + 1)
                link(dve.reciprocal(rs2[:, 2, t:t + 1], rs2[:, 1, t:t + 1]))
                dve.scalar_tensor_tensor(rs2[:, 3, t:t + 1], mv2[:, t, 0:1], -1.0, rs2[:, 2, t:t + 1], ALU.mult,
                                         ALU.mult).then_inc(s_nmr2, 1)
            low_x2(T - 2)
            low_x2(T - 1)
            dve.wait_ge(s_b1T, 1)
            dve.tensor_copy(b1col[:], psS[:, 256:256 + NX * FC]).then_inc(s_b1c, 1)

            for g, (t0, t1) in enumerate(TG):
                dve.wait_ge(s_lg, g + 1)
                cols = LG[:, t0 * TP:t1 * TP]
                dve.tensor_reduce(mx[:, g:g + 1], cols, AX.X, ALU.max)
                last = dve.tensor_reduce(mx[:, 4 + g:5 + g], cols, AX.X, ALU.min)
            link(last)
            dve.tensor_reduce(sel[:, 0:1], mx[:, 0:len(TG)], AX.X, ALU.max)
            link(dve.tensor_reduce(lows[:, 0, 0:1], mx[:, 4:4 + len(TG)], AX.X, ALU.min))
            dve.tensor_scalar(sel[:, 1:2], sel[:, 0:1], -1.0, None, ALU.mult).then_inc(s_max, 1)
            dve.tensor_tensor(sel[:, 3:4], sel[:, 0:1], lows[:, 0, 0:1], ALU.subtract)
            link(dve.scalar_tensor_tensor(sel[:, 4:5], lows[:, 0, 0:1], -1.0, sel[:, 0:1], ALU.mult, ALU.max))
            link(dve.tensor_scalar(sel[:, 4:5], sel[:, 4:5], 1e-6, 1e-25, ALU.mult, ALU.add))
            link(dve.scalar_tensor_tensor(sel[:, 5:6], sel[:, 3:4], 1.001, sel[:, 4:5], ALU.mult, ALU.add))
            link(dve.tensor_scalar(lows[:, 0, 1:2], sel[:, 5:6], 1.0 / G16, None, ALU.mult))
            for r in range(ROUNDS):
                link(dve.scalar_tensor_tensor(cnt[:, r, 0:1], jcol[:, 0:1], lows[:, r, 1:2], lows[:, r, 0:1], ALU.mult,
                                              ALU.add))
                link(dve.tensor_scalar(GE[:], LG[:], cnt[:, r, 0:1], None, ALU.is_ge, ALU.add, accum_out=cnt[:, r, 1:2]))
                dve.tensor_scalar(cnt[:, r, 2:3], cnt[:, r, 1:2], float(CAP), -1.0 / G16, ALU.is_ge,
                                  ALU.add).then_inc(s_ind, 1)
                link(dve.tensor_scalar(lows[:, r + 1, 1:2], lows[:, r, 1:2], 1.0 / G16, None, ALU.mult))
                dve.wait_ge(s_m16, r + 1)
                link(dve.scalar_tensor_tensor(lows[:, r + 1, 0:1], psS[:, 300 + r:301 + r], lows[:, r, 1:2],
                                              lows[:, r, 0:1], ALU.mult, ALU.add))
            low_t, step = lows[:, ROUNDS, 0:1], lows[:, ROUNDS - 1, 1:2]
            link(dve.scalar_tensor_tensor(sel[:, 10:11], low_t, -1.0, low_t, ALU.mult, ALU.max))
            link(dve.scalar_tensor_tensor(sel[:, 11:12], sel[:, 10:11], 1.2e-7, low_t, ALU.mult, ALU.add))
            link(dve.scalar_tensor_tensor(sel[:, 6:7], step, 2.0, sel[:, 11:12], ALU.mult, ALU.add))
            link(dve.tensor_scalar(GE[:], LG[:], sel[:, 6:7], None, ALU.is_ge, ALU.add, accum_out=sel[:, 7:8]))
            link(dve.scalar_tensor_tensor(CL[:], LG[:], low_t, GE[:], ALU.is_ge, ALU.subtract))
            link(dve.tensor_scalar(sel[:, 8:9], sel[:, 7:8], -1.0, float(CAP), ALU.mult, ALU.add))
            dve.wait_ge(s_exp, 1)
            link(dve.tensor_tensor_scan(LG[:], CL[:], CL[:], 0.0, ALU.add, ALU.bypass))
            link(dve.scalar_tensor_tensor(LG[:], LG[:], sel[:, 8:9], CL[:], ALU.is_le, ALU.mult))
            link(dve.tensor_tensor(LG[:], LG[:], GE[:], ALU.add))
            link(dve.reciprocal(sel[:, 9:10], sel[:, 2:3]))
            dve.scalar_tensor_tensor(EX[:], EX[:], sel[:, 9:10], LG[:], ALU.mult, ALU.mult).then_inc(s_w, 1)
            for g, (t0, t1) in enumerate(TG):
                dve.wait_ge(s_wT, g + 1)
                dve.tensor_copy(wtok[:, t0:t1, :],
                                O4[g + 1][0:TP, 0:(t1 - t0) * P].rearrange("p (t e j) -> p t e j", e=NX,
                                                                           j=G16)[:, :, :, 0]).then_inc(s_wtok, 1)
            dve.wait_ge(s_b2h, 2)
            dve.scalar_tensor_tensor(b2m[:], b2h[:].bitcast(F32), jm[:, 3:4], b2z[:], ALU.mult, ALU.add
                                     ).then_inc(s_b2m, 1)
            dve.wait_ge(s_wtok, 3)
            for e in range(NX):
                for t in range(T):
                    n = e * T + t
                    if n < NU:
                        dve.wait_ge(s_u, n + 1)
                    else:
                        dve.wait_ge(s_mm2, n + 1)
                    if e >= 1:
                        dve.wait_ge(s_acc, n - T + 1)
                    if e == 2:
                        dve.wait_ge(s_b2a, min(t + 1, T - 1))
                    elif e == 3:
                        dve.wait_ge(s_b2a, T)
                    res = U[:, t, :] if n < NU else O4[n % 4][0:TP, :]
                    dve.scalar_tensor_tensor(X1[:, t, :], res, wtok[:, t, e:e + 1], X1[:, t, :],
                                             ALU.mult, ALU.add).then_inc(s_acc, 1)
                    if n == NU - 1:
                        dve.wait_ge(s_exh, 2)
                        dve.scalar_tensor_tensor(EXm[:], EXh[:].bitcast(F32), jm[:, 1:2], LG[:], ALU.mult, ALU.add
                                                 ).then_inc(s_exm, 1)
                    if e in (1, 2) and t % 2 == 1:
                        k = (e - 1) * T // 2 + t // 2
                        dve.wait_ge(s_b2p, k + 1)
                        dve.wait_ge(s_acc, e * T + k + 1 if k <= t else (e - 1) * T + k + 1)
                        dve.tensor_tensor(X1[:, k, :], X1[:, k, :], psB, ALU.add).then_inc(s_b2a, 1)

        @block.tensor
        def _(pe):
            pe.wait_ge(s_diag, 1)
            pe.wait_ge(s_const, 1)
            pe.matmul(psS[0:TP, 0:TP], ones16[0:TP, 0:TP], diag16[:], start=True, stop=True).then_inc(s_rowps, 1)
            pe.wait_ge(s_gb, 16)
            pe.wait_ge(s_ident, 2)
            pe.wait_ge(s_rr, 1)
            pe.transpose(psS[:, 256:256 + KC], gb4[:], ident[0:KC, 0:KC]).then_inc(s_gbT, 1)

            for c in range(KC):
                if c >= 2:
                    pe.wait_ge(s_lo, c - 1)
                for o in range(KC):
                    pe.wait_ge(s_wscale, o + 1)
                    last = pe.transpose(TR[c % 2][:, o * P:(o + 1) * P], Wn[:, o, c * P:(c + 1) * P], ident[:])
                last.then_inc(s_tr, 1)
            def rows(k):
                pe.wait_ge(s_wscale, KC + 1)
                pe.wait_ge(s_const, 3)
                pe.wait_ge((s_kps_read, s_bcv)[k], (1, 2)[k])
                for c in range(KC):
                    last = pe.matmul(psS[0:TP, c * P:(c + 1) * P], ones[:, 0:TP], dscale[:, k, c, :], start=True, stop=True)
                last.then_inc(s_bc, 1)

            def turn(t):
                pe.wait_ge(s_xn, t + 1)
                pe.wait_ge(s_lo, KC + t - 1)
                for c in range(KC):
                    last = pe.transpose(TR[t % 2][:, c * TP:(c + 1) * TP], HB[:, t, c * P:(c + 1) * P],
                                        ident[0:TP, 0:TP])
                last.then_inc(s_tr, 1)

            def project(t):
                pe.wait_ge(s_lo, KC + t + 1)
                if t >= 2:
                    pe.wait_ge(s_hb, t - 1)
                for n, (a, w) in enumerate(((XNh, WTh), (XNl, WTh), (XNh, WTl))):
                    for c in range(KC):
                        last = pe.matmul(H[t % 2][0:TP, :], a[:, t % 2, c, :], w[:, c, :],
                                         start=(n == 0 and c == 0), stop=False)
                if t == 0:
                    pe.wait_ge(s_bcv, 2)
                for k in range(2):
                    last = pe.matmul(H[t % 2][0:TP, :], onesr[:, 0:TP], brow[:, k, :], start=False, stop=(k == 1))
                last.then_inc(s_h, 1)

            pe.wait_ge(s_ek, 2)
            for k in range(2):
                for h in range(HC):
                    to = (k * HC + h) * (NW + 1)
                    last = pe.transpose(psS16[:, to:to + NW], ek16[:, k, h * P:(h + 1) * P], ident16[0:NW, 0:NW])
            last.then_inc(s_kps, 1)
            turn(0)
            turn(1)
            rows(0)
            for t in range(T):
                project(t)
                if t == 0:
                    rows(1)
                if t + 2 < T:
                    turn(t + 2)

            pe.wait_ge(s_m, TP)
            pe.wait_ge(s_pad, 1)
            pe.wait_ge(s_hb, T)
            for b in range(NB):
                pe.wait_ge(s_n, sum(n0 < (b + 1) * CB for n0, _ in NPARTS[:2]))
                for k, (g0, g1) in enumerate(SETS):
                    if b:
                        pe.wait_ge(s_at, 2 * b - 1 + k)
                    for g in range(g0, g1):
                        for w in range(GW):
                            for h in range(HC):
                                i = (g * GW + w) * HC + h
                                if b * CB + i == NROOM:
                                    pe.wait_ge(s_n, len(NPARTS))
                                last = pe.matmul(AB[k][:, g - g0, w * NK:(w + 1) * NK], OHM[:, :, b * CB + i],
                                                 OHN[:, :, (b * CB + i) % NROOM], start=(h == 0), stop=(h == HC - 1))
                    last.then_inc(s_set, 1)

            pe.wait_ge(s_tot, 1)
            pe.matmul(psS[0:1, 0:1], tot[:, 0:1], ones[0:TP, 0:1], start=True, stop=True).then_inc(s_totps, 1)
            pe.wait_ge(s_flag, 1)
            general = pe.value_load(flag[0:1, 0:1], min_val=0, max_val=1)
            with pe.If(general):
                DC = N // 5
                pe.matmul(psS[0:1, 0:1], tot[:, 0:1], ones[0:TP, 0:1], start=True, stop=True).then_inc(s_gmm, 1)
                with pe.Fori(0, T) as q:
                    with pe.Fori(0, 5) as d:
                        group = q * 5 + d
                        pe.wait_ge(s_gev, group + 1)
                        pe.wait_ge(s_goh, group * (ROW // 2) + 1)
                        pe.matmul(psS[0:TP, 0:DC], ohs[:, 0, 0:TP], ohd[:, 0, :], start=True, stop=False,
                                  skip_group_check=True)
                        pe.matmul(psS[0:TP, 0:DC], ohs[:, 1, 0:TP], ohd[:, 1, :], start=False, stop=False,
                                  skip_group_check=True).then_inc(s_gmm, 1)
                        with pe.Fori(1, ROW // 2) as c:
                            pe.wait_ge(s_goh, group * (ROW // 2) + c + 1)
                            pe.matmul(psS[0:TP, 0:DC], ohs[:, 0, 0:TP], ohd[:, 0, :], start=False, stop=False,
                                      skip_group_check=True)
                            pe.matmul(psS[0:TP, 0:DC], ohs[:, 1, 0:TP], ohd[:, 1, :], start=False, stop=False,
                                      skip_group_check=True).then_inc(s_gmm, 1)
            pe.wait_ge(s_counts, 1)
            pe.wait_ge(s_own, T)
            pe.wait_ge(s_b1, 16)
            pe.transpose(psS[:, 256:256 + NX * FC], b1row[:], ident[0:NX * FC, 0:NX * FC]).then_inc(s_b1T, 1)

            def aggregate(*tiles):
                for q in range(T):
                    for t in tiles:
                        cols = slice(t * TP, (t + 1) * TP)
                        if q == 0 and t >= 2:
                            pe.wait_ge(s_res, t - 1)
                        for n, part in enumerate((HDh, HDl)):
                            if t == 0:
                                pe.wait_ge((s_hdh, s_hdl)[n], q + 1)
                            if q == T - 1 and n == 1:
                                with pe.If(general):
                                    for q2 in range(T):
                                        for part2 in (HDh, HDl):
                                            pe.matmul(H[t % 2][0:TP, :], AT2[0:TP, q2, cols], part2[:, q2, :],
                                                      start=False, stop=False, skip_group_check=True)
                            last = pe.matmul(H[t % 2][0:TP, :], AT[0:TP, q, cols], part[:, q, :],
                                             start=(q == 0 and n == 0), stop=(q == T - 1 and n == 1))
                        if q == T - 1:
                            last.then_inc(s_agg, 1)

            def turn2(t):
                pe.wait_ge(s_xn2, t + 1)
                if t >= 2:
                    pe.wait_ge(s_lo2, t - 1)
                for c in range(KC):
                    last = pe.transpose(TR[t % 2][:, c * TP:(c + 1) * TP], xn2[:, t % 2, c * P:(c + 1) * P],
                                        ident[0:TP, 0:TP])
                last.then_inc(s_tr2, 1)

            def logits(g):
                t0, t1 = TG[g]
                pe.wait_ge(s_lo2, t1)
                pe.wait_ge(s_wrs, 1)
                if g:
                    pe.wait_ge(s_res, T)
                cols = slice(t0 * TP, t1 * TP)
                for n, (w, a) in enumerate(((Wrh, XTh), (Wrl, XTh), (Wrh, XTl))):
                    for c in range(KC):
                        last = pe.matmul(LP[g][:, 0:(t1 - t0) * TP], w[:, c, :, :].rearrange("p e j -> p (e j)"),
                                         a[:, c, cols], start=(n == 0 and c == 0), stop=(n == 2 and c == KC - 1))
                last.then_inc(s_lgp, 1)

            def hidden_piece(e, i, rounds=()):
                f, a, b = PIECES[i]
                n = e * NP + i
                if n == 0:
                    pe.wait_ge(s_w1l, 1)
                elif n == 2:
                    pe.wait_ge(s_lg, 1)
                elif n >= 3:
                    pe.wait_ge(s_gelu, n - 2)
                for k, (w, z) in enumerate(((W1h, XTh), (W1l, XTh), (W1h, XTl))):
                    for c in range(KC):
                        last = pe.matmul(psX[:, i % 3, 0:b - a], w[e % 2][:, c, f * P:(f + 1) * P],
                                         z[:, c, a:b], start=(k == 0 and c == 0), stop=(k == 2 and c == KC - 1))
                        if (k * KC + c) in rounds:
                            r = rounds[k * KC + c]
                            pe.wait_ge(s_ind, r + 1)
                            pe.matmul(psS[:, 300 + r:301 + r], blk[:], cnt[:, r, 2:3], start=True, stop=True
                                      ).then_inc(s_m16, 1)
                last.then_inc(s_mm1, 1)

            def hidden_layer(e):
                pe.wait_ge(s_w1l, e + 1)
                for i in range(NP):
                    hidden_piece(e, i)

            aggregate(0, 1)
            for t in range(2, T):
                aggregate(t)
                turn2(t - 2)
            logits(0)
            turn2(T - 2)
            hidden_piece(0, 0)
            turn2(T - 1)
            logits(1)
            logits(2)

            def output_layer(e, t0=0, t1=T):
                pe.wait_ge(s_w2l, e + 1)
                pe.wait_ge(s_hl, NP * (e + 1))
                for t in range(t0, t1):
                    n = e * T + t
                    if 4 <= n < NU:
                        pe.wait_ge(s_u, n - 3)
                    elif n == NU:
                        pe.wait_ge(s_u, NU)
                        pe.wait_ge(s_wtok, 3)
                    elif n >= NU + 4:
                        pe.wait_ge(s_acc, n - 3)
                    for k, (z, w) in enumerate(((Hh, W2h), (Hl, W2h), (Hh, W2l))):
                        for f in range(FC):
                            last = pe.matmul(O4[n % 4][0:TP, :], z[:, e % 2, f, t * TP:(t + 1) * TP],
                                             w[e % 2][:, f, :], start=(k == 0 and f == 0), stop=(k == 2 and f == FC - 1))
                    last.then_inc(s_mm2, 1)
                    if e in (1, 2) and t % 2 == 1:
                        k = (e - 1) * T // 2 + t // 2
                        if k == 0:
                            pe.wait_ge(s_exm, 1)
                            pe.wait_ge(s_b2m, 1)
                        else:
                            pe.wait_ge(s_b2a, k)
                        pe.matmul(psB, EXm[:, k * TP:(k + 1) * TP], b2m[:], start=True, stop=True).then_inc(s_b2p, 1)

            pe.wait_ge(s_blk, 4)
            for n in range(1, 2 * NP):
                if n == NP:
                    pe.wait_ge(s_w1l, 2)
                hidden_piece(n // NP, n % NP, TURNS.get(n, {}))
            output_layer(0, 0, NU)
            pe.wait_ge(s_w, 1)
            for g, (t0, t1) in enumerate(TG):
                pe.wait_ge(s_u, g + 2)
                for t in range(t0, t1):
                    last = pe.transpose(O4[g + 1][0:TP, (t - t0) * P:(t - t0 + 1) * P], EX[:, t * TP:(t + 1) * TP],
                                        ident[:])
                last.then_inc(s_wT, 1)
            for e in range(NX):
                output_layer(e, 0 if e else NU)
                if e + 2 < NX:
                    hidden_layer(e + 2)


_INS = ['x', 'src', 'dst', 'L0_gnn_W', 'L0_gnn_b', 'L0_ffn_Wr', 'L0_ffn_W1', 'L0_ffn_b1', 'L0_ffn_W2', 'L0_ffn_b2']


def kernel(**inputs):
    import concourse.bacc as _bacc
    from concourse.bass_utils import run_bass_kernel_spmd as _run

    nc = _bacc.Bacc("TRN2", target_bir_lowering=False, num_devices=1)
    arrays, args = {}, []
    for name in _INS:
        a = np.ascontiguousarray(inputs[name])
        arrays[f"in_{name}"] = a
        args.append(nc.dram_tensor(f"in_{name}", a.shape, mybir.dt.from_np(a.dtype), kind="ExternalInput").ap())
    args.append(nc.dram_tensor("out", inputs["x"].shape, F32, kind="ExternalOutput").ap())
    gnn_ffn(nc, *args)
    return _run(nc, [arrays], core_ids=[0]).results[0]["out"]
```

```python
from contextlib import ExitStack

import numpy as np

import concourse.bass as bass
from concourse import mybir

ALU = mybir.AluOpType
ACT = mybir.ActivationFunctionType
AX = mybir.AxisListType
F32 = mybir.dt.float32
F32R = mybir.dt.float32r
F16 = mybir.dt.float16
I32 = mybir.dt.int32

P = 128
EPS = 1e-5
ROUND = 12582912.0


def gnn_ffn(nc, x, src, dst, gnn_W, gnn_b, Wr, W1, b1, W2, b2, out):
    N, D = x.shape
    E = src.shape[0]
    NX, _, F = W1.shape
    KC = D // P
    FC = F // P
    TP = 125
    T = N // TP
    CAP = min(512, N)
    ROW = E // TP

    WIN = 10
    NW = N // WIN
    HC = 3
    SLOT = HC * P
    NCH = NW * HC
    NB = 5
    WB = NW // NB
    CB = WB * HC
    GW = 5
    KEYS = WIN + 2
    NK = T * WIN
    SETS = [(0, 3), (3, 5)]
    NROOM = 272
    NPARTS = [(0, 2 * CB), (2 * CB, NROOM), (NROOM, NCH)]
    HSCALE = 16384.0
    G16 = 16
    ROUNDS = 7
    SPLIT = [(0, 120), (120, TP)]
    NU = 5
    TG = [(0, 4), (4, 8), (8, 10)]
    assert T * TP == N and TP * ROW == E and NX * G16 == P and NW <= P and NB * WB == NW

    with ExitStack() as ctx:
        def sb(name, shape, dt):
            return ctx.enter_context(nc.sbuf_tensor(name, shape, dt))

        def sem(name):
            return ctx.enter_context(nc.semaphore(name))

        ident = sb("ident", [P, P], F32)
        ident16 = sb("ident16", [P, P], F16)
        ones = sb("ones", [P, P], F32)
        ones16 = sb("ones16", [P, P], F16)
        blk = sb("blk", [P, P], F32)
        win0 = sb("win0", [P, 1], F32)
        rowid = sb("rowid", [P, 1], F32)
        jm = sb("jm", [P, 4], F32)
        jcol = sb("jcol", [P, 3], F32)
        dst_e = sb("dst_e", [TP, ROW], I32)
        src_e = sb("src_e", [TP, ROW], I32)
        diag16 = sb("diag16", [TP, TP], F16)
        sm = sb("sm", [P, 16], F32)
        smi = sb("smi", [P, 4], I32)
        junk = sb("junk", [P, 1], F32)
        keyM = sb("keyM", [P, NCH + 1], F16)
        keyN = sb("keyN", [P, NCH + 1], F16)
        bn = sb("bn", [TP, T, 6], F32)
        mv = sb("mv", [TP, T, 2], F32)
        rstd = sb("rstd", [TP, 3, T], F32)
        nmr = sb("nmr", [TP, T], F32)
        wsc = sb("wsc", [P, 8, KC], F32)
        gb4 = sb("gb4", [KC, P], F32)
        degp = sb("degp", [TP, T, NB * 2], F32)
        dis = sb("dis", [TP, 4, T], F32)
        tot = sb("tot", [TP, 2], F32)
        flag = sb("flag", [1, 2], I32)
        bn2 = sb("bn2", [TP, 2, 6], F32)
        mv2 = sb("mv2", [TP, T, 2], F32)
        rs2 = sb("rs2", [TP, 4, T], F32)
        b1row = sb("b1row", [NX * FC, P], F32)
        b1col = sb("b1col", [P, (NX + 2) * FC], F32)
        b1now = sb("b1now", [P, 2, FC], F32)
        mx = sb("mx", [P, 8], F32)
        sel = sb("sel", [P, 16], F32)
        cnt = sb("cnt", [P, ROUNDS, 4], F32)
        lows = sb("lows", [P, ROUNDS + 1, 2], F32)
        wtok = sb("wtok", [TP, T, NX], F32)
        inv_bc = sb("inv_bc", [TP, D], F32)
        onesr = sb("onesr", [1, P], F32R)
        brow = sb("brow", [1, 2, D], F32R)

        base = (nc.sbuf_base + 63) // 64 * 64
        plan = {}

        def at(name, shape, dt, off):
            size = int(np.prod(shape[1:])) * (2 if dt == F16 else 4)
            plan[name] = (off, off + size)
            return nc.alloc_sbuf_tensor_at(name, shape, dt, offset=base + off)

        def end(name):
            return (plan[name][1] + 63) // 64 * 64

        AT = at("AT", [P, T, N + 6], F16, 0)
        XNh = at("XNh", [P, 2, KC, TP], F32R, 0)
        XNl = at("XNl", [P, 2, KC, TP], F32R, end("XNh"))
        WTh = at("WTh", [P, KC, D], F32R, end("XNl"))
        WTl = at("WTl", [P, KC, D], F32R, end("WTh"))
        assert end("WTl") <= end("AT")
        HB = at("HB", [TP, T, D], F32, end("AT"))
        OHM = at("OHM", [P, P, NCH], F16, end("HB"))
        OHN = at("OHN", [P, NK, NROOM], F16, end("OHM"))
        room = nc.sbuf_usable_end - base
        Wn = at("Wn", [P, KC, D], F32, plan["OHN"][0])
        Wsq = at("Wsq", [P, D], F32, end("Wn"))
        grow = at("grow", [TP, ROW], I32, end("Wsq"))
        grow16 = at("grow16", [TP, ROW], F16, end("grow"))
        gd = at("gd", [NW, SLOT], I32, end("grow16"))
        gs = at("gs", [NW, SLOT], I32, end("gd"))
        ek = at("ek", [NW, 4, SLOT], F32, end("gs"))
        ek16 = at("ek16", [NW, 2, SLOT], F16, end("ek"))
        dscale = at("dscale", [P, 2, KC, P], F32, end("ek16"))
        cmp16 = at("cmp16", [TP, ROW], F16, end("dscale"))
        assert end("cmp16") <= end("OHN")
        HDh = at("HDh", [TP, T, D], F16, plan["OHN"][0])
        HDl = at("HDl", [TP, T, D], F16, end("HDh"))
        AT2 = at("AT2", [P, T, N + 6], F16, end("HDl"))
        dst_f = at("dst_f", [TP, ROW], F32, plan["OHM"][0])
        src_f = at("src_f", [TP, ROW], F32, end("dst_f"))
        srcq_f = at("srcq_f", [TP, ROW], F32, end("src_f"))
        iota_n = at("iota_n", [TP, N], F32, end("srcq_f"))
        ohs = at("ohs", [TP, 2, P], F16, end("iota_n"))
        ohd = at("ohd", [TP, 2, N // 5], F16, end("ohs"))
        atp = at("atp", [TP, N // 5], F32, end("ohd"))
        assert end("AT2") <= room
        X1 = at("X1", [TP, T, D], F32, plan["OHM"][0])
        XTh = at("XTh", [P, KC, N], F32R, end("X1"))
        XTl = at("XTl", [P, KC, N], F32R, end("XTh"))
        xn2 = at("xn2", [TP, 2, D], F32, end("XTl"))
        WrN = at("WrN", [P, KC, NX], F32, end("xn2"))
        Wrh = at("Wrh", [P, KC, NX, G16], F32R, end("WrN"))
        Wrl = at("Wrl", [P, KC, NX, G16], F32R, end("Wrh"))
        LG = at("LG", [P, N], F32, end("Wrl"))
        b2z = at("b2z", [P, D], F32, end("LG"))
        W1n = at("W1n", [P, 2, KC, F], F32, end("b2z"))
        W2n = at("W2n", [P, 2, FC, D], F32, end("W1n"))
        assert end("W2n") <= plan["OHN"][0], (end("W2n"), plan["OHN"][0])
        W1h, W1l, W2h, W2l = [], [], [], []
        for n, off in enumerate((plan["HB"][0], plan["OHN"][0])):
            W1h.append(at(f"W1h{n}", [P, KC, F], F32R, off))
            W1l.append(at(f"W1l{n}", [P, KC, F], F32R, end(f"W1h{n}")))
            W2h.append(at(f"W2h{n}", [P, FC, D], F32R, end(f"W1l{n}")))
            W2l.append(at(f"W2l{n}", [P, FC, D], F32R, end(f"W2h{n}")))
        Hh = at("Hh", [P, 2, FC, N], F32R, 0)
        HG = at("HG", [P, 2, 512], F32, end("W2l0"))
        assert end("Hh") <= plan["HB"][0] and end("HG") <= plan["OHM"][0]
        Hl = at("Hl", [P, 2, FC, N], F32R, end("W2l1"))
        EX = at("EX", [P, N], F32, end("Hl"))
        GE = at("GE", [P, N], F16, end("EX"))
        U = at("U", [TP, NU, D], F32, end("GE"))
        assert end("U") <= room, (end("U"), room)
        CL = at("CL", [P, N], F16, end("Hh"))
        EXh = at("EXh", [P, N], F32R, end("Hh"))
        assert end("EXh") <= plan["HB"][0]
        EXm = at("EXm", [P, N], F32R, plan["LG"][0])
        b2h = at("b2h", [P, D], F32R, plan["xn2"][0])
        b2m = at("b2m", [P, D], F32R, end("b2h"))
        assert end("b2m") <= end("xn2")

        banks = [ctx.enter_context(nc.psum_tensor(f"bank{i}", [P, 512], F32)) for i in range(3)]
        TR = banks[0:2]
        psX = ctx.enter_context(nc.psum_tensor("psX", [P, 3, 512], F32))
        psY = ctx.enter_context(nc.psum_tensor("psY", [P, 2, 512], F32))
        H = [banks[2], psY[:, 0, :]]
        O4 = [banks[0], banks[1], banks[2], psY[:, 0, :]]
        psB = [psX[0:TP, 2, :], psY[0:TP, 1, :]]
        psS = psY[:, 1, :]
        LP = [psX[:, 2, :], psY[:, 0, :], banks[2]]
        psS16 = psS.bitcast(F16)
        AB = [psX, psY]

        s_dst = sem("s_dst")
        s_x = [sem(f"s_x{i}") for i in range(5)]
        s_W = sem("s_W")
        s_gb = sem("s_gb")
        s_ident = sem("s_ident")
        s_const = sem("s_const")
        s_link = sem("s_link")
        s_diag = sem("s_diag")
        s_rowps = sem("s_rowps")
        s_rr = sem("s_rr")
        s_grow = sem("s_grow")
        s_start = sem("s_start")
        s_gath = sem("s_gath")
        s_ek = sem("s_ek")
        s_kps = sem("s_kps")
        s_kps_read = sem("s_kps_read")
        s_ssq = sem("s_ssq")
        s_gbT = sem("s_gbT")
        s_wroot = sem("s_wroot")
        s_wscale = sem("s_wscale")
        s_var = sem("s_var")
        s_std = sem("s_std")
        s_nmr = sem("s_nmr")
        s_xn = sem("s_xn")
        s_tr = sem("s_tr")
        s_hi = sem("s_hi")
        s_lo = sem("s_lo")
        s_bc = sem("s_bc")
        s_dscale = sem("s_dscale")
        s_browh = sem("s_browh")
        s_inv = sem("s_inv")
        s_bcv = sem("s_bcv")
        s_h = sem("s_h")
        s_hb = sem("s_hb")
        s_pad = sem("s_pad")
        s_blk = sem("s_blk")
        s_m = sem("s_m")
        s_n = sem("s_n")
        s_set = sem("s_set")
        s_at = sem("s_at")
        s_at2 = sem("s_at2")
        s_own = sem("s_own")
        s_src = sem("s_src")
        s_gsrc = sem("s_gsrc")
        s_gp = sem("s_gp")
        s_gend = sem("s_gend")
        s_tot = sem("s_tot")
        s_totps = sem("s_totps")
        s_flag = sem("s_flag")
        s_giota = sem("s_giota")
        s_goh = sem("s_goh")
        s_gmm = sem("s_gmm")
        s_gev = sem("s_gev")
        s_counts = sem("s_counts")
        s_droot = sem("s_droot")
        s_dis = sem("s_dis")
        s_hdh = sem("s_hdh")
        s_hdl = sem("s_hdl")
        s_x1 = [sem(f"s_x1{i}") for i in range(5)]
        s_agg = sem("s_agg")
        s_res = sem("s_res")
        s_var2 = sem("s_var2")
        s_std2 = sem("s_std2")
        s_nmr2 = sem("s_nmr2")
        s_xn2 = sem("s_xn2")
        s_tr2 = sem("s_tr2")
        s_hi2 = sem("s_hi2")
        s_lo2 = sem("s_lo2")
        s_Wr = sem("s_Wr")
        s_b1 = sem("s_b1")
        s_b2 = sem("s_b2")
        s_b2z = sem("s_b2z")
        s_b1T = sem("s_b1T")
        s_b1c = sem("s_b1c")
        s_b1n = sem("s_b1n")
        s_wrs = sem("s_wrs")
        s_lgp = sem("s_lgp")
        s_lg = sem("s_lg")
        s_max = sem("s_max")
        s_exp = sem("s_exp")
        s_ind = sem("s_ind")
        s_m16 = sem("s_m16")
        s_w = sem("s_w")
        s_wT = sem("s_wT")
        s_wtok = sem("s_wtok")
        s_b2p = sem("s_b2p")
        s_b2a = sem("s_b2a")
        s_b2h = sem("s_b2h")
        s_b2m = sem("s_b2m")
        s_exm = sem("s_exm")
        s_exh = sem("s_exh")
        s_u = sem("s_u")
        s_jm = sem("s_jm")
        s_w1n = [sem("s_w1n0"), sem("s_w1n1")]
        s_w2n = [sem("s_w2n0"), sem("s_w2n1")]
        s_w1h = sem("s_w1h")
        s_w2h = sem("s_w2h")
        s_w1l = sem("s_w1l")
        s_w2l = sem("s_w2l")
        s_mm1 = sem("s_mm1")
        s_gelu = sem("s_gelu")
        s_hh = sem("s_hh")
        s_hl = sem("s_hl")
        s_mm2 = sem("s_mm2")
        s_acc = sem("s_acc")
        s_out = sem("s_out")
        sets = len(SETS)
        OUT = [(0, 2), (2, 4), (4, 6), (6, 8), (8, 9), (9, 10)]
        PIECES = [(f, a, b) for a, b in ((0, 500), (500, 1000), (1000, N)) for f in range(FC)]
        TURNS = {2: {5: 0, 11: 1}, 5: {2: 2}, 6: {7: 3}, 7: {7: 4}, 8: {4: 5}, 9: {3: 6}}
        NP = len(PIECES)

        x_v = x.rearrange("(t p) d -> p t d", p=TP)
        out_v = out.rearrange("(t p) d -> p t d", p=TP)
        dst_v = dst.rearrange("(r c) -> r c", c=ROW)
        src_v = src.rearrange("(r c) -> r c", c=ROW)

        block = ctx.enter_context(nc.Block())

        @block.sync
        def _(sp):
            for a, b in SPLIT:
                sp.dma_start(dst_e[a:b, :], dst_v[a:b, :]).then_inc(s_dst, 16)
            for i in range(5):
                if i == 1:
                    sp.wait_ge(s_grow, 16)
                for a, b in SPLIT:
                    sp.dma_start(HB[a:b, 2 * i:2 * i + 2, :], x_v[a:b, 2 * i:2 * i + 2, :]).then_inc(s_x[i], 16)

            for a, b in SPLIT:
                sp.dma_start(src_e[a:b, :], src_v[a:b, :]).then_inc(s_src, 16)
            sp.dma_start(b1row[:], b1.rearrange("e (f p) -> (e f) p", p=P)).then_inc(s_b1, 16)
            sp.wait_ge(s_counts, 1)
            for i in range(5):
                for a, b in SPLIT:
                    sp.dma_start(X1[a:b, 2 * i:2 * i + 2, :], x_v[a:b, 2 * i:2 * i + 2, :]).then_inc(s_x1[i], 16)
                if i == 0:
                    sp.dma_start(WrN[:], Wr.rearrange("(c p) e -> p c e", p=P)).then_inc(s_Wr, 16)
            def load(e, odd, first):
                w1, w2 = (W[e] if first else W[bass.ds(e, 1)].rearrange("a r c -> (a r) c") for W in (W1, W2))
                if not first:
                    sp.wait_ge(s_w1l, e - 1)
                    sp.wait_ge(s_w1h, e - 1)
                sp.dma_start(W1n[:, odd, :, :], w1.rearrange("(c p) f -> p c f", p=P)).then_inc(s_w1n[odd], 16)
                if not first:
                    sp.wait_ge(s_w2l, e - 1)
                    sp.wait_ge(s_w2h, e - 1)
                sp.dma_start(W2n[:, odd, :, :], w2.rearrange("(c p) d -> p c d", p=P)).then_inc(s_w2n[odd], 16)

            load(0, 0, True)
            sp.wait_ge(s_b2z, 1)
            for j in range(3):
                sp.dma_start(b2z[j:P:G16, :], b2).then_inc(s_b2, 16)
            load(1, 1, True)
            with sp.Fori(1, NX // 2) as pair:
                load(pair * 2, 0, False)
                load(pair * 2 + 1, 1, False)
            for t0, t1 in OUT:
                sp.wait_ge(s_acc, (NX - 1) * T + t1)
                for a, b in SPLIT:
                    sp.dma_start(out_v[a:b, t0:t1, :], X1[a:b, t0:t1, :]).then_inc(s_out, 16)
            sp.wait_ge(s_out, 16 * 2 * len(OUT))
            sp.wait_ge(s_src, 32)

        @block.gpsimd
        def _(pool):
            pool.memset(ident[:], 0.0).then_inc(s_ident, 1)
            pool.memset(ones16[:], 1.0).then_inc(s_const, 1)
            pool.wait_ge(s_ident, 1)
            pool.affine_select(out=ident[:], in_=ident[:], compare_op=ALU.not_equal, fill=1.0, base=0,
                               pattern=[[-1, P]], channel_multiplier=1).then_inc(s_ident, 1)
            pool.iota(win0[:], pattern=[[0, 1]], base=0, channel_multiplier=WIN,
                      allow_small_or_imprecise_dtypes=True).then_inc(s_const, 1)
            pool.memset(ones[:], 1.0).then_inc(s_const, 1)
            pool.memset(OHM[:, TP:P, :].rearrange("p a c -> p (a c)"), 0.0).then_inc(s_pad, 1)
            pool.wait_ge(s_rr, 1)
            pool.indirect_dma_start(out=grow[:], out_offset=None, in_=dst_v,
                                    in_offset=bass.IndirectOffsetOnAxis(ap=smi[0:TP, 0:1], axis=0)
                                    ).then_inc(s_grow, 16)
            pool.wait_ge(s_start, 1)
            for lst, to in ((dst, gd), (src, gs)):
                pool.indirect_dma_start(out=to[:], out_offset=None, in_=lst.rearrange("(a n) -> a n", a=1),
                                        in_offset=bass.IndirectOffsetOnAxis(ap=smi[0:NW, 1:2], axis=1)
                                        ).then_inc(s_gath, 16)

            pool.memset(blk[:], 1.0).then_inc(s_blk, 1)
            pool.iota(rowid[:], pattern=[[0, 1]], base=0, channel_multiplier=1,
                      allow_small_or_imprecise_dtypes=True).then_inc(s_blk, 1)
            blk_v = blk[:].rearrange("p (g j) -> p g j", j=G16)
            pool.wait_ge(s_blk, 2)
            pool.affine_select(out=blk_v, in_=blk_v, compare_op=ALU.is_ge, fill=0.0, base=0,
                               pattern=[[-G16, NX], [0, G16]], channel_multiplier=1).then_inc(s_blk, 1)
            pool.wait_ge(s_blk, 3)
            pool.affine_select(out=blk_v, in_=blk_v, compare_op=ALU.is_ge, fill=0.0, base=G16 - 1,
                               pattern=[[G16, NX], [0, G16]], channel_multiplier=-1).then_inc(s_blk, 1)

            for b in range(NB):
                pool.wait_ge(s_at, min(2 * b + 2, 2 * NB - 1))
                if b == NB - 1:
                    pool.wait_ge(s_at2, 1)
                for t in (2 * b, 2 * b + 1):
                    own = AT[0:TP, t, t * TP:(t + 1) * TP]
                    pool.tensor_tensor(own, own, ident16[0:TP, 0:TP], ALU.add).then_inc(s_own, 1)

            pool.wait_ge(s_flag, 1)
            general = pool.value_load(flag[0:1, 0:1], min_val=0, max_val=1)
            with pool.If(general):
                pool.iota(iota_n[:], pattern=[[1, N]], base=0, channel_multiplier=0,
                          allow_small_or_imprecise_dtypes=True).then_inc(s_giota, 1)

            pool.wait_ge(s_counts, 1)
            pool.memset(b2z[:], 0.0).then_inc(s_b2z, 1)

            def low(to, full, high, done):
                pool.tensor_tensor(to, full, high.bitcast(F32), ALU.subtract).then_inc(done, 1)

            def low_w1(e, odd, first=False):
                if not first:
                    pool.wait_ge(s_mm1, (e - 1) * NP)
                pool.wait_ge(s_w1h, e + 1)
                low(W1l[odd][:], W1n[:, odd, :, :], W1h[odd][:], s_w1l)

            def low_w2(e, odd, first=False):
                if not first:
                    pool.wait_ge(s_mm2, (e - 1) * T)
                pool.wait_ge(s_w2h, e + 1)
                low(W2l[odd][:], W2n[:, odd, :, :], W2h[odd][:], s_w2l)

            def low_hidden(e, odd, first=False):
                for i, (f, a, b) in enumerate(PIECES):
                    pool.wait_ge(s_hh, e * NP + (i + 1))
                    if not first:
                        pool.wait_ge(s_mm2, (e - 1) * T)
                    low(Hl[:, odd, f, a:b], HG[:, i % 2, 0:b - a], Hh[:, odd, f, a:b], s_hl)

            for n in range(2):
                pool.wait_ge(s_w1n[n], 16)
                low_w1(n, n, True)
                if n == 0:
                    pool.wait_ge(s_w2n[n], 16)
                    low_w2(n, n, True)
            low_hidden(0, 0, True)
            low_w2(1, 1, True)
            low_w1(2, 0)
            low_hidden(1, 1, True)
            low_w2(2, 0)
            low_w1(3, 1)
            with pool.Fori(1, NX // 2 - 1) as pair:
                e = pair * 2
                low_hidden(e, 0)
                low_w2(e + 1, 1)
                low_w1(e + 2, 0)
                low_hidden(e + 1, 1)
                low_w2(e + 2, 0)
                low_w1(e + 3, 1)
            low_hidden(NX - 2, 0)
            low_w2(NX - 1, 1)
            low_hidden(NX - 1, 1)

        @block.scalar
        def _(act):
            act.dma_start(Wn[:], gnn_W.rearrange("(c p) i -> p c i", p=P)).then_inc(s_W, 16)
            act.dma_start(gb4[:], gnn_b.rearrange("(c p) -> c p", p=P)).then_inc(s_gb, 16)
            act.wait_ge(s_W, 16)
            for c in range(KC):
                if c:
                    act.wait_ge(s_ssq, c)
                act.activation(Wsq[:], Wn[:, c, :], ACT.Square, accum_out=wsc[:, 0, c:c + 1]).then_inc(s_ssq, 1)
            act.wait_ge(s_ssq, KC)
            act.activation(wsc[:, 1, :], wsc[:, 0, :], ACT.Sqrt, scale=float(D)).then_inc(s_wroot, 1)

            def root(g):
                act.wait_ge(s_var, g + 1)
                act.activation(rstd[:, 1, 2 * g:2 * g + 2], rstd[:, 0, 2 * g:2 * g + 2], ACT.Sqrt).then_inc(s_std, 1)

            def norm(t):
                act.wait_ge(s_nmr, t // 2 + 1)
                act.activation(HB[:, t, :], HB[:, t, :], ACT.Identity, bias=nmr[:, t:t + 1],
                               scale=rstd[:, 2, t:t + 1]).then_inc(s_xn, 1)

            def high_w(c):
                act.wait_ge(s_tr, c + 1)
                act.activation(WTh[:, c, :], TR[c % 2][:], ACT.Copy).then_inc(s_hi, 1)

            def high_x(t):
                act.wait_ge(s_tr, KC + t + 1)
                if t >= 2:
                    act.wait_ge(s_h, t - 1)
                act.activation(XNh[:, t % 2, :, :].rearrange("p a c -> p (a c)"), TR[t % 2][:, 0:KC * TP],
                               ACT.Copy).then_inc(s_hi, 1)

            def hidden(t):
                act.wait_ge(s_h, t + 1)
                act.activation(HB[:, t, :], H[t % 2][0:TP, :], ACT.Copy).then_inc(s_hb, 1)

            root(0)
            high_w(0)
            high_w(1)
            norm(0)
            norm(1)
            high_w(2)
            high_w(3)
            root(1)
            act.wait_ge(s_ident, 2)
            for c in range(KC):
                act.activation(dscale[:, 0, c, :], ident[:], ACT.Copy, scale=wsc[:, 7, c:c + 1])
                last = act.activation(dscale[:, 1, c, :], ident[:], ACT.Copy, scale=wsc[:, 5, c:c + 1])
            last.then_inc(s_dscale, 1)
            for t in range(T):
                high_x(t)
                if t == 0:
                    act.wait_ge(s_bc, 1)
                    act.activation(brow[:, 0, :], psS[0:1, :], ACT.Copy).then_inc(s_browh, 1)
                if t == 2:
                    act.wait_ge(s_bc, 2)
                    act.activation(inv_bc[:], psS[0:TP, :], ACT.Copy).then_inc(s_inv, 1)
                if t + 2 < T:
                    norm(t + 2)
                if t < 3:
                    root(t + 2)
                if t >= 1:
                    hidden(t - 1)
            hidden(T - 1)

            for b in range(NB):
                for k, (g0, g1) in enumerate(SETS):
                    if 2 * b + k == 2 * NB - 2:
                        continue
                    act.wait_ge(s_set, 2 * b + k + 1)
                    ps = AB[k][0:TP, :, 0:GW * NK].rearrange("p g (w q d) -> p q g w d", q=T, d=WIN)
                    d0 = (b * 5 + g0) * GW * WIN
                    for q in range(T):
                        to = AT[0:TP, q, d0:d0 + (g1 - g0) * GW * WIN].rearrange("p (g w d) -> p g w d", w=GW, d=WIN)
                        last = act.activation(to, ps[:, q], ACT.Copy, accum_out=degp[:, q, 2 * b + k:2 * b + k + 1])
                    last.then_inc(s_at, 1)

            act.wait_ge(s_counts, 1)
            act.activation(dis[:, 2, :], dis[:, 1, :], ACT.Sqrt).then_inc(s_droot, 1)
            act.wait_ge(s_dis, 1)
            for t in range(T):
                act.activation(HDh[:, t, :], HB[:, t, :], ACT.Copy, scale=dis[:, 3, t:t + 1]).then_inc(s_hdh, 1)

            def high_w1(e, odd, first=False):
                if not first:
                    act.wait_ge(s_mm1, (e - 1) * NP)
                elif e == 0:
                    act.wait_ge(s_hdl, T)
                else:
                    act.wait_ge(s_agg, T)
                act.wait_ge(s_w1n[odd], 16 if first else (e - odd) * 8 + 16)
                act.activation(W1h[odd][:], W1n[:, odd, :, :], ACT.Copy).then_inc(s_w1h, 1)

            def high_w2(e, odd, first=False):
                if not first:
                    act.wait_ge(s_mm2, (e - 1) * T)
                act.wait_ge(s_w2n[odd], 16 if first else (e - odd) * 8 + 16)
                act.activation(W2h[odd][:], W2n[:, odd, :, :], ACT.Copy).then_inc(s_w2h, 1)

            def root2(t):
                act.wait_ge(s_var2, t + 1)
                act.activation(rs2[:, 1, t:t + 1], rs2[:, 0, t:t + 1], ACT.Sqrt).then_inc(s_std2, 1)

            def norm2(t):
                act.wait_ge(s_nmr2, t + 1)
                if t >= 2:
                    act.wait_ge(s_tr2, t - 1)
                act.activation(xn2[:, t % 2, :], X1[:, t, :], ACT.Identity, bias=rs2[:, 3, t:t + 1],
                               scale=rs2[:, 2, t:t + 1]).then_inc(s_xn2, 1)

            def high_x2(t):
                act.wait_ge(s_tr2, t + 1)
                act.activation(XTh[:, :, t * TP:(t + 1) * TP],
                               TR[t % 2][:, 0:KC * TP].rearrange("p (c n) -> p c n", c=KC), ACT.Copy).then_inc(s_hi2, 1)

            for t in range(T):
                if t >= 2:
                    high_x2(t - 2)
                root2(t)
                norm2(t)
                if t == 4:
                    high_w1(0, 0, True)
                if t == 5:
                    high_w2(0, 0, True)
            high_x2(T - 2)
            high_x2(T - 1)
            for g, (t0, t1) in enumerate(TG):
                act.wait_ge(s_lgp, g + 1)
                act.activation(LG[:, t0 * TP:t1 * TP], LP[g][:, 0:(t1 - t0) * TP], ACT.Copy).then_inc(s_lg, 1)
            act.wait_ge(s_max, 1)
            act.activation(EX[:], LG[:], ACT.Exp, bias=sel[:, 1:2], accum_out=sel[:, 2:3]).then_inc(s_exp, 1)
            high_w1(1, 1, True)
            act.wait_ge(s_b2, 48)
            act.wait_ge(s_tr2, T)
            act.wait_ge(s_jm, 1)
            act.activation(b2h[:], b2z[:], ACT.Copy).then_inc(s_b2h, 1)
            act.wait_ge(s_b2h, 1)
            act.activation(b2z[:], b2z[:], ACT.Copy, scale=jm[:, 2:3]).then_inc(s_b2h, 1)

            act.wait_ge(s_b1c, 2)
            def gelu(e, odd, first=False):
                for i, (f, a, b) in enumerate(PIECES):
                    n = e * NP + i
                    act.wait_ge(s_mm1, n + 1)
                    if not (first and e == 0 and i < 2):
                        act.wait_ge(s_hl, n - 1)
                    if not first:
                        act.wait_ge(s_mm2, (e - 1) * T)
                        act.wait_ge(s_b1n, e - 1)
                    bias = b1col[:, e * FC + f:e * FC + f + 1] if first else b1now[:, odd, f:f + 1]
                    act.activation(HG[:, i % 2, 0:b - a], psX[:, i % 3, 0:b - a], ACT.Gelu,
                                   bias=bias).then_inc(s_gelu, 1)
                    act.wait_ge(s_gelu, n + 1)
                    act.activation(Hh[:, odd, f, a:b], HG[:, i % 2, 0:b - a], ACT.Copy).then_inc(s_hh, 1)

            gelu(0, 0, True)
            high_w2(1, 1, True)
            high_w1(2, 0)
            gelu(1, 1, True)
            for t in range(NU):
                act.wait_ge(s_mm2, t + 1)
                act.activation(U[:, t, :], O4[t % 4][0:TP, :], ACT.Copy).then_inc(s_u, 1)
            act.wait_ge(s_w, 1)
            act.activation(EXh[:], EX[:], ACT.Copy).then_inc(s_exh, 1)
            act.activation(LG[:], EX[:], ACT.Copy, scale=jm[:, 0:1]).then_inc(s_exh, 1)
            high_w2(2, 0)
            high_w1(3, 1)
            with act.Fori(1, NX // 2 - 1) as pair:
                e = pair * 2
                gelu(e, 0)
                high_w2(e + 1, 1)
                high_w1(e + 2, 0)
                gelu(e + 1, 1)
                high_w2(e + 2, 0)
                high_w1(e + 3, 1)
            gelu(NX - 2, 0)
            high_w2(NX - 1, 1)
            gelu(NX - 1, 1)

        @block.vector
        def _(dve):
            chain = [0]

            def link(ins):
                chain[0] += 1
                ins.then_inc(s_link, 1)
                dve.wait_ge(s_link, chain[0])

            dve.wait_ge(s_ident, 2)
            link(dve.tensor_copy(ident16[:], ident[:]))
            dve.wait_ge(s_dst, 32)
            dve.tensor_scalar(diag16[:], ident16[0:TP, 0:TP], dst_e[:, 0:1], None, ALU.mult).then_inc(s_diag, 1)

            def stats(t):
                dve.wait_ge(s_x[t // 2], 32)
                link(dve.bn_stats(bn[:, t, :], HB[:, t, :]))
                link(dve.bn_aggr(mv[:, t, :], bn[:, t, :]))

            def variances(g):
                a, b = 2 * g, 2 * g + 2
                dve.tensor_scalar(rstd[:, 0, a:b], mv[:, a:b, 1], EPS, None, ALU.add).then_inc(s_var, 1)

            def scales(g):
                a, b = 2 * g, 2 * g + 2
                dve.wait_ge(s_std, g + 1)
                link(dve.reciprocal(rstd[:, 2, a:b], rstd[:, 1, a:b]))
                dve.scalar_tensor_tensor(nmr[:, a:b], mv[:, a:b, 0], -1.0, rstd[:, 2, a:b], ALU.mult,
                                         ALU.mult).then_inc(s_nmr, 1)

            dve.wait_ge(s_rowps, 1)
            dve.wait_ge(s_const, 3)
            link(dve.tensor_scalar(cmp16[0:TP, 0:TP], psS[0:TP, 0:TP], win0[0:TP, :], None, ALU.is_lt, ALU.add,
                                   accum_out=sm[0:TP, 0:1]))
            link(dve.tensor_scalar(sm[0:TP, 1:2], sm[0:TP, 0:1], -1.0, 0.0, ALU.add, ALU.max))
            dve.tensor_copy(smi[0:TP, 0:1], sm[0:TP, 1:2]).then_inc(s_rr, 1)
            for t in range(2):
                stats(t)
            variances(0)
            dve.wait_ge(s_grow, 16)
            link(dve.tensor_copy(grow16[:], grow[:]))
            link(dve.tensor_scalar(cmp16[:], grow16[:], win0[0:TP, :], None, ALU.is_lt, ALU.add,
                                   accum_out=sm[0:TP, 2:3]))
            link(dve.scalar_tensor_tensor(sm[0:TP, 3:4], sm[0:TP, 1:2], float(ROW), sm[0:TP, 2:3], ALU.mult, ALU.add))
            link(dve.tensor_scalar(sm[0:TP, 4:5], sm[0:TP, 3:4], float(E - SLOT), None, ALU.min))
            dve.tensor_copy(smi[0:NW, 1:2], sm[0:NW, 4:5]).then_inc(s_start, 1)

            dve.wait_ge(s_gbT, 1)
            link(dve.tensor_scalar(wsc[:, 2, :], psS[:, 256:256 + KC], -1.0, None, ALU.mult))
            link(dve.tensor_tensor(wsc[:, 3, :], psS[:, 256:256 + KC], wsc[:, 2, :], ALU.max))
            dve.wait_ge(s_wroot, 1)
            link(dve.scalar_tensor_tensor(wsc[:, 4, :], wsc[:, 1, :], 1e-30, wsc[:, 3, :], ALU.add, ALU.add))
            link(dve.tensor_scalar(wsc[:, 5, :], wsc[:, 4, :], 1.0 / HSCALE, None, ALU.mult))
            link(dve.reciprocal(wsc[:, 6, :], wsc[:, 5, :]))
            link(dve.scalar_tensor_tensor(wsc[:, 7, :], wsc[:, 2, :], -1.0, wsc[:, 6, :], ALU.mult, ALU.mult))
            for c in range(KC):
                dve.tensor_scalar(Wn[:, c, :], Wn[:, c, :], wsc[:, 6, c:c + 1], None, ALU.mult).then_inc(s_wscale, 1)
            def pair(g):
                stats(2 * g)
                stats(2 * g + 1)
                variances(g)

            def low_w(c):
                dve.wait_ge(s_hi, c + 1)
                dve.tensor_tensor(WTl[:, c, :], TR[c % 2][:], WTh[:, c, :].bitcast(F32), ALU.subtract).then_inc(s_lo, 1)

            low_w(0)
            scales(0)
            low_w(1)
            pair(1)

            dve.wait_ge(s_gath, 32)
            link(dve.tensor_scalar(ek[:, 0, :], gd[:], win0[0:NW, :], None, ALU.subtract))
            link(dve.tensor_scalar(ek[:, 0, :], ek[:, 0, :], -1.0, float(WIN), ALU.max, ALU.min))
            link(dve.tensor_scalar(ek[:, 1, :], gs[:], 1.0 / TP, 0.5 / TP - 0.5, ALU.mult, ALU.add))
            link(dve.tensor_scalar(ek[:, 2, :], ek[:, 1, :], ROUND, -ROUND, ALU.add, ALU.add))
            dve.scalar_tensor_tensor(ek16[:, 0, :], ek[:, 2, :], -float(TP), gs[:], ALU.mult, ALU.add).then_inc(s_ek, 1)
            dve.scalar_tensor_tensor(ek16[:, 1, :], ek[:, 2, :], float(KEYS), ek[:, 0, :], ALU.mult,
                                     ALU.add).then_inc(s_ek, 1)

            def low_x(t):
                dve.wait_ge(s_hi, KC + t + 1)
                dve.tensor_tensor(XNl[:, t % 2, :, :].rearrange("p a c -> p (a c)"), TR[t % 2][:, 0:KC * TP],
                                  XNh[:, t % 2, :, :].rearrange("p a c -> p (a c)").bitcast(F32),
                                  ALU.subtract).then_inc(s_lo, 1)

            def bias_row():
                dve.tensor_copy(onesr[:], ones[0:1, :]).then_inc(s_bcv, 1)
                dve.wait_ge(s_browh, 1)
                dve.tensor_tensor(brow[:, 1, :], psS[0:1, :], brow[:, 0, :].bitcast(F32),
                                  ALU.subtract).then_inc(s_bcv, 1)

            low_w(2)
            low_w(3)
            dve.wait_ge(s_kps, 1)
            for k, to in ((0, keyM), (1, keyN)):
                last = dve.tensor_copy(to[:, 0:NCH].rearrange("p (w h) -> p h w", h=HC),
                                       psS16[:, k * HC * (NW + 1):(k + 1) * HC * (NW + 1)].rearrange(
                                           "p (h w) -> p h w", h=HC)[:, :, 0:NW])
            link(last)
            dve.tensor_copy(junk[:, 0:1], win0[:]).then_inc(s_kps_read, 1)

            between = {1: (low_x, 0), 3: (scales, 1), 6: (pair, 2), 9: (bias_row,), 13: (low_x, 1), 18: (pair, 3),
                       24: (scales, 2), 28: (pair, 4), 30: (scales, 3), 36: (low_x, 2),
                       40: (scales, 4), 54: (low_x, 3), 71: (low_x, 4), 88: (low_x, 5), 105: (low_x, 6),
                       122: (low_x, 7), TP + 26: (low_x, 8), TP + 53: (low_x, 9)}

            def aside(j):
                if j in between:
                    step, *which = between[j]
                    step(*which)

            for j in range(TP):
                last = dve.tensor_scalar(OHM[:, j, :], keyM[:, 0:NCH], float(j), None, ALU.is_equal)
                if j < TP - 1:
                    aside(j)
            last.then_inc(s_m, 1)
            for n0, n1 in NPARTS:
                if n0 == NROOM:
                    dve.wait_ge(s_set, 4)
                for n in range(NK):
                    key = float(n // WIN * KEYS + n % WIN)
                    last = dve.tensor_scalar(OHN[:, n, n0 % NROOM:(n1 - 1) % NROOM + 1], keyN[:, n0:n1], key, None,
                                             ALU.is_equal)
                    if n0 == 0:
                        aside(TP + n)
                last.then_inc(s_n, 1)

            dve.wait_ge(s_set, 2 * NB - 1)
            ps = psX[0:TP, :, 0:GW * NK].rearrange("p g (w q d) -> p q g w d", q=T, d=WIN)
            g0, g1 = SETS[0]
            d0 = (NB - 1) * 5 * GW * WIN
            for q in range(T):
                to = AT[0:TP, q, d0:d0 + (g1 - g0) * GW * WIN].rearrange("p (g w d) -> p g w d", w=GW, d=WIN)
                last = dve.tensor_scalar(to, ps[:, q], 1.0, None, ALU.mult, ALU.add,
                                         accum_out=degp[:, q, 2 * NB - 2:2 * NB - 1])
            last.then_inc(s_at2, 1)
            dve.wait_ge(s_at2, 1)
            dve.wait_ge(s_at, 2 * NB - 1)
            link(dve.tensor_reduce(dis[:, 0, :], degp[:], AX.X, ALU.add))
            dve.tensor_reduce(tot[:, 0:1], dis[:, 0, :], AX.X, ALU.add).then_inc(s_tot, 1)
            link(dve.tensor_scalar(dis[:, 1, :], dis[:, 0, :], 1.0, None, ALU.add))
            dve.wait_ge(s_totps, 1)
            dve.tensor_scalar(flag[:, 0:1], psS[0:1, 0:1], float(E), None, ALU.not_equal).then_inc(s_flag, 1)
            dve.wait_ge(s_flag, 1)
            general = dve.value_load(flag[0:1, 0:1], min_val=0, max_val=1)
            with dve.If(general):
                dve.wait_ge(s_src, 32)
                dve.wait_ge(s_giota, 1)
                dve.wait_ge(s_own, T)
                dve.tensor_copy(dst_f[:], dst_e[:]).then_inc(s_gev, 1)
                dve.tensor_copy(src_f[:], src_e[:]).then_inc(s_gsrc, 1)
                DC = N // 5
                with dve.Fori(0, T) as q:
                    dve.wait_ge(s_gsrc, q + 1)
                    dve.wait_ge(s_gmm, q * (5 * ROW // 2) + 1)
                    dve.tensor_scalar(srcq_f[:], src_f[:], iota_n[:, bass.ds(q * TP, 1)], None,
                                      ALU.subtract).then_inc(s_gsrc, 1)
                    dve.wait_ge(s_gsrc, q + 2)
                    dve.tensor_copy(junk[:, 0:1], win0[:])
                    with dve.Fori(0, 5) as d:
                        with dve.Fori(0, ROW // 2) as c:
                            step = (q * 5 + d) * (ROW // 2) + c
                            dve.wait_ge(s_gmm, step + 1)
                            for k in range(2):
                                dve.tensor_scalar(ohs[:, k, 0:TP], iota_n[:, 0:TP], srcq_f[:, bass.ds(c * 2 + k, 1)],
                                                  None, ALU.is_equal)
                                last = dve.tensor_scalar(ohd[:, k, :], iota_n[:, bass.ds(d * DC, DC)],
                                                         dst_f[:, bass.ds(c * 2 + k, 1)], None, ALU.is_equal)
                            last.then_inc(s_goh, 1)
                        group = q * 5 + d
                        dve.wait_ge(s_gmm, (group + 1) * (ROW // 2) + 1)
                        dve.tensor_copy(atp[:], psS[0:TP, 0:DC]).then_inc(s_gp, 1)
                        dve.wait_ge(s_gp, group * 2 + 1)
                        part = AT[0:TP, bass.ds(q, 1), bass.ds(d * DC, DC)].rearrange("p a n -> p (a n)")
                        part2 = AT2[0:TP, bass.ds(q, 1), bass.ds(d * DC, DC)].rearrange("p a n -> p (a n)")
                        dve.tensor_copy(part, atp[:]).then_inc(s_gp, 1)
                        dve.wait_ge(s_gp, group * 2 + 2)
                        dve.tensor_tensor(part2, atp[:], part, ALU.subtract).then_inc(s_gev, 1)
                dve.wait_ge(s_gev, 5 * T + 1)
                for t in range(T):
                    own = AT2[0:TP, t, t * TP:(t + 1) * TP]
                    last = dve.tensor_tensor(own, own, ident16[0:TP, 0:TP], ALU.add)
                last.then_inc(s_gend, 1)
                dve.wait_ge(s_gend, 1)
                dve.tensor_reduce(dis[:, 0, :], AT[0:TP, :, 0:N], AX.X, ALU.add)
                dve.tensor_reduce(dis[:, 2, :], AT2[0:TP, :, 0:N], AX.X, ALU.add).then_inc(s_gend, 1)
                dve.wait_ge(s_gend, 2)
                dve.tensor_tensor(dis[:, 1, :], dis[:, 0, :], dis[:, 2, :], ALU.add).then_inc(s_gend, 1)
                dve.wait_ge(s_gend, 3)
            dve.tensor_copy(junk[:, 0:1], win0[:]).then_inc(s_counts, 1)

            dve.wait_ge(s_droot, 1)
            dve.reciprocal(dis[:, 3, :], dis[:, 2, :]).then_inc(s_dis, 1)
            dve.wait_ge(s_dis, 1)
            for t in range(T):
                dve.wait_ge(s_hdh, t + 1)
                dve.scalar_tensor_tensor(HDl[:, t, :], HB[:, t, :], dis[:, 3, t:t + 1], HDh[:, t, :], ALU.mult,
                                         ALU.subtract).then_inc(s_hdl, 1)

            dve.wait_ge(s_Wr, 16)
            wide = WrN[:].unsqueeze(3).to_broadcast([P, KC, NX, G16])
            link(dve.tensor_copy(Wrh[:], wide))
            dve.tensor_tensor(Wrl[:], wide, Wrh[:].bitcast(F32), ALU.subtract).then_inc(s_wrs, 1)
            dve.wait_ge(s_blk, 2)
            link(dve.tensor_scalar(jcol[:, 1:2], rowid[:], 1.0 / G16, 0.5 / G16 - 0.5, ALU.mult, ALU.add))
            link(dve.tensor_scalar(jcol[:, 2:3], jcol[:, 1:2], ROUND, -ROUND, ALU.add, ALU.add))
            link(dve.scalar_tensor_tensor(jcol[:, 0:1], jcol[:, 2:3], -float(G16), rowid[:], ALU.mult, ALU.add))

            for j in range(2):
                link(dve.tensor_scalar(jm[:, 2 * j:2 * j + 1], jcol[:, 0:1], float(j + 1), None, ALU.is_equal))
                last = dve.tensor_scalar(jm[:, 2 * j + 1:2 * j + 2], jm[:, 2 * j:2 * j + 1], -2.0, 1.0, ALU.mult,
                                         ALU.add)
            last.then_inc(s_jm, 1)

            def low_x2(t):
                dve.wait_ge(s_hi2, t + 1)
                to = XTl[:, :, t * TP:(t + 1) * TP]
                dve.tensor_tensor(to, TR[t % 2][:, 0:KC * TP].rearrange("p (c n) -> p c n", c=KC),
                                  XTh[:, :, t * TP:(t + 1) * TP].bitcast(F32), ALU.subtract).then_inc(s_lo2, 1)

            for t in range(T):
                dve.wait_ge(s_agg, t + 1)
                dve.wait_ge(s_x1[t // 2], 32)
                if t >= 2:
                    dve.wait_ge(s_tr2, t - 1)
                if t == 0:
                    dve.wait_ge(s_inv, 1)
                tmp = xn2[:, t % 2, :]
                dve.scalar_tensor_tensor(tmp, H[t % 2][0:TP, :], 0.0, inv_bc[:], ALU.max, ALU.mult).then_inc(s_res, 1)
                dve.wait_ge(s_res, t + 1)
                link(dve.scalar_tensor_tensor(X1[:, t, :], tmp, dis[:, 3, t:t + 1], X1[:, t, :], ALU.mult, ALU.add))
                link(dve.bn_stats(bn2[:, t % 2, :], X1[:, t, :]))
                link(dve.bn_aggr(mv2[:, t, :], bn2[:, t % 2, :]))
                dve.tensor_scalar(rs2[:, 0, t:t + 1], mv2[:, t, 1:2], EPS, None, ALU.add).then_inc(s_var2, 1)
                if t >= 2:
                    low_x2(t - 2)
                dve.wait_ge(s_std2, t + 1)
                link(dve.reciprocal(rs2[:, 2, t:t + 1], rs2[:, 1, t:t + 1]))
                dve.scalar_tensor_tensor(rs2[:, 3, t:t + 1], mv2[:, t, 0:1], -1.0, rs2[:, 2, t:t + 1], ALU.mult,
                                         ALU.mult).then_inc(s_nmr2, 1)
            low_x2(T - 2)
            low_x2(T - 1)
            dve.wait_ge(s_b1T, 1)
            dve.memset(b1col[:, NX * FC:(NX + 2) * FC], 0.0).then_inc(s_b1c, 1)
            dve.tensor_copy(b1col[:, 0:NX * FC], psS[:, 256:256 + NX * FC]).then_inc(s_b1c, 1)

            for g, (t0, t1) in enumerate(TG):
                dve.wait_ge(s_lg, g + 1)
                cols = LG[:, t0 * TP:t1 * TP]
                dve.tensor_reduce(mx[:, g:g + 1], cols, AX.X, ALU.max)
                last = dve.tensor_reduce(mx[:, 4 + g:5 + g], cols, AX.X, ALU.min)
            link(last)
            dve.tensor_reduce(sel[:, 0:1], mx[:, 0:len(TG)], AX.X, ALU.max)
            link(dve.tensor_reduce(lows[:, 0, 0:1], mx[:, 4:4 + len(TG)], AX.X, ALU.min))
            dve.tensor_scalar(sel[:, 1:2], sel[:, 0:1], -1.0, None, ALU.mult).then_inc(s_max, 1)
            dve.tensor_tensor(sel[:, 3:4], sel[:, 0:1], lows[:, 0, 0:1], ALU.subtract)
            link(dve.scalar_tensor_tensor(sel[:, 4:5], lows[:, 0, 0:1], -1.0, sel[:, 0:1], ALU.mult, ALU.max))
            link(dve.tensor_scalar(sel[:, 4:5], sel[:, 4:5], 1e-6, 1e-25, ALU.mult, ALU.add))
            link(dve.scalar_tensor_tensor(sel[:, 5:6], sel[:, 3:4], 1.001, sel[:, 4:5], ALU.mult, ALU.add))
            link(dve.tensor_scalar(lows[:, 0, 1:2], sel[:, 5:6], 1.0 / G16, None, ALU.mult))
            for r in range(ROUNDS):
                link(dve.scalar_tensor_tensor(cnt[:, r, 0:1], jcol[:, 0:1], lows[:, r, 1:2], lows[:, r, 0:1], ALU.mult,
                                              ALU.add))
                link(dve.tensor_scalar(GE[:], LG[:], cnt[:, r, 0:1], None, ALU.is_ge, ALU.add,
                                       accum_out=cnt[:, r, 1:2]))
                dve.tensor_scalar(cnt[:, r, 2:3], cnt[:, r, 1:2], float(CAP), -1.0 / G16, ALU.is_ge,
                                  ALU.add).then_inc(s_ind, 1)
                link(dve.tensor_scalar(lows[:, r + 1, 1:2], lows[:, r, 1:2], 1.0 / G16, None, ALU.mult))
                dve.wait_ge(s_m16, r + 1)
                link(dve.scalar_tensor_tensor(lows[:, r + 1, 0:1], psS[:, 300 + r:301 + r], lows[:, r, 1:2],
                                              lows[:, r, 0:1], ALU.mult, ALU.add))
            low_t, step = lows[:, ROUNDS, 0:1], lows[:, ROUNDS - 1, 1:2]
            link(dve.scalar_tensor_tensor(sel[:, 10:11], low_t, -1.0, low_t, ALU.mult, ALU.max))
            link(dve.scalar_tensor_tensor(sel[:, 11:12], sel[:, 10:11], 1.2e-7, low_t, ALU.mult, ALU.add))
            link(dve.scalar_tensor_tensor(sel[:, 6:7], step, 2.0, sel[:, 11:12], ALU.mult, ALU.add))
            link(dve.tensor_scalar(GE[:], LG[:], sel[:, 6:7], None, ALU.is_ge, ALU.add, accum_out=sel[:, 7:8]))
            link(dve.scalar_tensor_tensor(CL[:], LG[:], low_t, GE[:], ALU.is_ge, ALU.subtract))
            link(dve.tensor_scalar(sel[:, 8:9], sel[:, 7:8], -1.0, float(CAP), ALU.mult, ALU.add))
            dve.wait_ge(s_exp, 1)
            link(dve.tensor_tensor_scan(LG[:], CL[:], CL[:], 0.0, ALU.add, ALU.bypass))
            link(dve.scalar_tensor_tensor(LG[:], LG[:], sel[:, 8:9], CL[:], ALU.is_le, ALU.mult))
            link(dve.tensor_tensor(LG[:], LG[:], GE[:], ALU.add))
            link(dve.reciprocal(sel[:, 9:10], sel[:, 2:3]))
            dve.scalar_tensor_tensor(EX[:], EX[:], sel[:, 9:10], LG[:], ALU.mult, ALU.mult).then_inc(s_w, 1)
            for g, (t0, t1) in enumerate(TG):
                dve.wait_ge(s_wT, g + 1)
                dve.tensor_copy(wtok[:, t0:t1, :],
                                O4[g + 1][0:TP, 0:(t1 - t0) * P].rearrange("p (t e j) -> p t e j", e=NX,
                                                                           j=G16)[:, :, :, 0]).then_inc(s_wtok, 1)
            dve.wait_ge(s_b2h, 2)
            dve.scalar_tensor_tensor(b2m[:], b2h[:].bitcast(F32), jm[:, 3:4], b2z[:], ALU.mult, ALU.add
                                     ).then_inc(s_b2m, 1)
            dve.wait_ge(s_wtok, 3)
            def weigh(e, odd, t, first=False):
                n = e * T + t
                unweighed = first and n < NU
                if unweighed:
                    dve.wait_ge(s_u, n + 1)
                else:
                    dve.wait_ge(s_mm2, n + 1)
                if not (first and e == 0):
                    dve.wait_ge(s_acc, n - T + 1)
                res = U[:, t, :] if unweighed else O4[(odd * T + t) % 4][0:TP, :]
                weight = wtok[:, t, e:e + 1] if first else wtok[:, t, bass.ds(e, 1)]
                dve.scalar_tensor_tensor(X1[:, t, :], res, weight, X1[:, t, :], ALU.mult, ALU.add).then_inc(s_acc, 1)

            def next_bias(e, odd, first=False):
                dve.wait_ge(s_gelu, e * NP + NP)
                cols = b1col[:, (e + 2) * FC:(e + 3) * FC] if first else b1col[:, bass.ds((e + 2) * FC, FC)]
                dve.tensor_scalar(b1now[:, odd, :], cols, 1.0, None, ALU.mult).then_inc(s_b1n, 1)

            dve.wait_ge(s_b1c, 2)
            next_bias(0, 0, True)
            for t in range(T):
                weigh(0, 0, t, True)
                if t == NU - 1:
                    dve.wait_ge(s_exh, 2)
                    dve.scalar_tensor_tensor(EXm[:], EXh[:].bitcast(F32), jm[:, 1:2], LG[:], ALU.mult, ALU.add
                                             ).then_inc(s_exm, 1)
            next_bias(1, 1, True)

            def add_b2(t):
                dve.wait_ge(s_b2p, t + 1)
                dve.wait_ge(s_acc, T + t + 1)
                dve.tensor_tensor(X1[:, t, :], X1[:, t, :], psB[t % 2], ALU.add).then_inc(s_b2a, 1)

            for t in range(T):
                weigh(1, 1, t, True)
                if t:
                    add_b2(t - 1)
            add_b2(T - 1)
            dve.wait_ge(s_b2a, T)
            with dve.Fori(1, NX // 2) as pair:
                for odd in range(2):
                    next_bias(pair * 2 + odd, odd)
                    for t in range(T):
                        weigh(pair * 2 + odd, odd, t)

        @block.tensor
        def _(pe):
            pe.wait_ge(s_diag, 1)
            pe.wait_ge(s_const, 1)
            pe.matmul(psS[0:TP, 0:TP], ones16[0:TP, 0:TP], diag16[:], start=True, stop=True).then_inc(s_rowps, 1)
            pe.wait_ge(s_gb, 16)
            pe.wait_ge(s_ident, 2)
            pe.wait_ge(s_rr, 1)
            pe.transpose(psS[:, 256:256 + KC], gb4[:], ident[0:KC, 0:KC]).then_inc(s_gbT, 1)

            for c in range(KC):
                if c >= 2:
                    pe.wait_ge(s_lo, c - 1)
                for o in range(KC):
                    pe.wait_ge(s_wscale, o + 1)
                    last = pe.transpose(TR[c % 2][:, o * P:(o + 1) * P], Wn[:, o, c * P:(c + 1) * P], ident[:])
                last.then_inc(s_tr, 1)
            def rows(k):
                pe.wait_ge(s_dscale, 1)
                pe.wait_ge(s_const, 3)
                pe.wait_ge((s_kps_read, s_bcv)[k], (1, 2)[k])
                for c in range(KC):
                    last = pe.matmul(psS[0:TP, c * P:(c + 1) * P], ones[:, 0:TP], dscale[:, k, c, :],
                                     start=True, stop=True)
                last.then_inc(s_bc, 1)

            def turn(t):
                pe.wait_ge(s_xn, t + 1)
                pe.wait_ge(s_lo, KC + t - 1)
                for c in range(KC):
                    last = pe.transpose(TR[t % 2][:, c * TP:(c + 1) * TP], HB[:, t, c * P:(c + 1) * P],
                                        ident[0:TP, 0:TP])
                last.then_inc(s_tr, 1)

            def project(t):
                pe.wait_ge(s_lo, KC + t + 1)
                if t >= 2:
                    pe.wait_ge(s_hb, t - 1)
                for n, (a, w) in enumerate(((XNh, WTh), (XNl, WTh), (XNh, WTl))):
                    for c in range(KC):
                        last = pe.matmul(H[t % 2][0:TP, :], a[:, t % 2, c, :], w[:, c, :],
                                         start=(n == 0 and c == 0), stop=False)
                if t == 0:
                    pe.wait_ge(s_bcv, 2)
                for k in range(2):
                    last = pe.matmul(H[t % 2][0:TP, :], onesr[:, 0:TP], brow[:, k, :], start=False, stop=(k == 1))
                last.then_inc(s_h, 1)

            pe.wait_ge(s_ek, 2)
            for k in range(2):
                for h in range(HC):
                    to = (k * HC + h) * (NW + 1)
                    last = pe.transpose(psS16[:, to:to + NW], ek16[:, k, h * P:(h + 1) * P], ident16[0:NW, 0:NW])
            last.then_inc(s_kps, 1)
            turn(0)
            turn(1)
            rows(0)
            for t in range(T):
                project(t)
                if t == 0:
                    rows(1)
                if t + 2 < T:
                    turn(t + 2)

            pe.wait_ge(s_m, 1)
            pe.wait_ge(s_pad, 1)
            pe.wait_ge(s_hb, T)
            for b in range(NB):
                pe.wait_ge(s_n, sum(n0 < (b + 1) * CB for n0, _ in NPARTS[:2]))
                for k, (g0, g1) in enumerate(SETS):
                    if b:
                        pe.wait_ge(s_at, 2 * b - 1 + k)
                    for g in range(g0, g1):
                        for w in range(GW):
                            for h in range(HC):
                                i = (g * GW + w) * HC + h
                                if b * CB + i == NROOM:
                                    pe.wait_ge(s_n, len(NPARTS))
                                last = pe.matmul(AB[k][:, g - g0, w * NK:(w + 1) * NK], OHM[:, :, b * CB + i],
                                                 OHN[:, :, (b * CB + i) % NROOM], start=(h == 0), stop=(h == HC - 1))
                    last.then_inc(s_set, 1)

            pe.wait_ge(s_tot, 1)
            pe.matmul(psS[0:1, 0:1], tot[:, 0:1], ones[0:TP, 0:1], start=True, stop=True).then_inc(s_totps, 1)
            pe.wait_ge(s_flag, 1)
            general = pe.value_load(flag[0:1, 0:1], min_val=0, max_val=1)
            with pe.If(general):
                DC = N // 5
                pe.matmul(psS[0:1, 0:1], tot[:, 0:1], ones[0:TP, 0:1], start=True, stop=True).then_inc(s_gmm, 1)
                with pe.Fori(0, T) as q:
                    with pe.Fori(0, 5) as d:
                        group = q * 5 + d
                        pe.wait_ge(s_gev, group + 1)
                        pe.wait_ge(s_goh, group * (ROW // 2) + 1)
                        pe.matmul(psS[0:TP, 0:DC], ohs[:, 0, 0:TP], ohd[:, 0, :], start=True, stop=False,
                                  skip_group_check=True)
                        pe.matmul(psS[0:TP, 0:DC], ohs[:, 1, 0:TP], ohd[:, 1, :], start=False, stop=False,
                                  skip_group_check=True).then_inc(s_gmm, 1)
                        with pe.Fori(1, ROW // 2) as c:
                            pe.wait_ge(s_goh, group * (ROW // 2) + c + 1)
                            pe.matmul(psS[0:TP, 0:DC], ohs[:, 0, 0:TP], ohd[:, 0, :], start=False, stop=False,
                                      skip_group_check=True)
                            pe.matmul(psS[0:TP, 0:DC], ohs[:, 1, 0:TP], ohd[:, 1, :], start=False, stop=False,
                                      skip_group_check=True).then_inc(s_gmm, 1)
            pe.wait_ge(s_counts, 1)
            pe.wait_ge(s_own, T)
            pe.wait_ge(s_b1, 16)
            pe.transpose(psS[:, 256:256 + NX * FC], b1row[:], ident[0:NX * FC, 0:NX * FC]).then_inc(s_b1T, 1)

            def aggregate(*tiles):
                for q in range(T):
                    for t in tiles:
                        cols = slice(t * TP, (t + 1) * TP)
                        if q == 0 and t >= 2:
                            pe.wait_ge(s_res, t - 1)
                        for n, part in enumerate((HDh, HDl)):
                            if t == 0:
                                pe.wait_ge((s_hdh, s_hdl)[n], q + 1)
                            if q == T - 1 and n == 1:
                                with pe.If(general):
                                    for q2 in range(T):
                                        for part2 in (HDh, HDl):
                                            pe.matmul(H[t % 2][0:TP, :], AT2[0:TP, q2, cols], part2[:, q2, :],
                                                      start=False, stop=False, skip_group_check=True)
                            last = pe.matmul(H[t % 2][0:TP, :], AT[0:TP, q, cols], part[:, q, :],
                                             start=(q == 0 and n == 0), stop=(q == T - 1 and n == 1))
                        if q == T - 1:
                            last.then_inc(s_agg, 1)

            def turn2(t):
                pe.wait_ge(s_xn2, t + 1)
                if t >= 2:
                    pe.wait_ge(s_lo2, t - 1)
                for c in range(KC):
                    last = pe.transpose(TR[t % 2][:, c * TP:(c + 1) * TP], xn2[:, t % 2, c * P:(c + 1) * P],
                                        ident[0:TP, 0:TP])
                last.then_inc(s_tr2, 1)

            def logits(g):
                t0, t1 = TG[g]
                pe.wait_ge(s_lo2, t1)
                pe.wait_ge(s_wrs, 1)
                if g:
                    pe.wait_ge(s_res, T)
                cols = slice(t0 * TP, t1 * TP)
                for n, (w, a) in enumerate(((Wrh, XTh), (Wrl, XTh), (Wrh, XTl))):
                    for c in range(KC):
                        last = pe.matmul(LP[g][:, 0:(t1 - t0) * TP], w[:, c, :, :].rearrange("p e j -> p (e j)"),
                                         a[:, c, cols], start=(n == 0 and c == 0), stop=(n == 2 and c == KC - 1))
                last.then_inc(s_lgp, 1)

            def hidden_piece(e, odd, i, rounds=(), first=False):
                f, a, b = PIECES[i]
                n = e * NP + i
                if not (first and e == 0):
                    if i == 0:
                        pe.wait_ge(s_w1l, e + 1)
                    pe.wait_ge(s_gelu, n - 2)
                elif i == 0:
                    pe.wait_ge(s_w1l, 1)
                elif i == 2:
                    pe.wait_ge(s_lg, 1)
                elif i >= 3:
                    pe.wait_ge(s_gelu, n - 2)
                for k, (w, z) in enumerate(((W1h, XTh), (W1l, XTh), (W1h, XTl))):
                    for c in range(KC):
                        last = pe.matmul(psX[:, i % 3, 0:b - a], w[odd][:, c, f * P:(f + 1) * P],
                                         z[:, c, a:b], start=(k == 0 and c == 0), stop=(k == 2 and c == KC - 1))
                        if (k * KC + c) in rounds:
                            r = rounds[k * KC + c]
                            pe.wait_ge(s_ind, r + 1)
                            pe.matmul(psS[:, 300 + r:301 + r], blk[:], cnt[:, r, 2:3], start=True, stop=True
                                      ).then_inc(s_m16, 1)
                last.then_inc(s_mm1, 1)

            def hidden_layer(e, odd):
                for i in range(NP):
                    hidden_piece(e, odd, i)

            aggregate(0, 1)
            for t in range(2, T):
                aggregate(t)
                turn2(t - 2)
            logits(0)
            turn2(T - 2)
            hidden_piece(0, 0, 0, first=True)
            turn2(T - 1)
            logits(1)
            logits(2)

            def output_tile(e, odd, t, wait):
                if wait:
                    pe.wait_ge(*wait)
                for k, (z, w) in enumerate(((Hh, W2h), (Hl, W2h), (Hh, W2l))):
                    for f in range(FC):
                        last = pe.matmul(O4[(odd * T + t) % 4][0:TP, :], z[:, odd, f, t * TP:(t + 1) * TP],
                                         w[odd][:, f, :], start=(k == 0 and f == 0), stop=(k == 2 and f == FC - 1))
                last.then_inc(s_mm2, 1)

            def output_layer(e, odd):
                pe.wait_ge(s_w2l, e + 1)
                pe.wait_ge(s_hl, e * NP + NP)
                for t in range(T):
                    output_tile(e, odd, t, (s_acc, e * T + (t - 3)))

            pe.wait_ge(s_blk, 4)
            for n in range(1, 2 * NP):
                hidden_piece(n // NP, n // NP, n % NP, TURNS.get(n, {}), first=True)
            pe.wait_ge(s_w2l, 1)
            pe.wait_ge(s_hl, NP)
            for t in range(NU):
                output_tile(0, 0, t, (s_u, t - 3) if t >= 4 else None)
            pe.wait_ge(s_w, 1)
            for g, (t0, t1) in enumerate(TG):
                pe.wait_ge(s_u, g + 2)
                for t in range(t0, t1):
                    last = pe.transpose(O4[g + 1][0:TP, (t - t0) * P:(t - t0 + 1) * P], EX[:, t * TP:(t + 1) * TP],
                                        ident[:])
                last.then_inc(s_wT, 1)
            pe.wait_ge(s_u, NU)
            for t in range(NU, T):
                output_tile(0, 0, t, (s_wtok, 3) if t < NU + 4 else (s_acc, t - 3))
            hidden_layer(2, 0)

            def b2_tile(t):
                if t == 0:
                    pe.wait_ge(s_gelu, 3 * NP)
                elif t >= 2:
                    pe.wait_ge(s_b2a, t - 1)
                pe.matmul(psB[t % 2], EXm[:, t * TP:(t + 1) * TP], b2m[:], start=True, stop=True).then_inc(s_b2p, 1)

            pe.wait_ge(s_w2l, 2)
            pe.wait_ge(s_hl, 2 * NP)
            pe.wait_ge(s_exm, 1)
            pe.wait_ge(s_b2m, 1)
            for t in range(T):
                output_tile(1, 1, t, (s_acc, T + t - 3))
                if t:
                    b2_tile(t - 1)
            b2_tile(T - 1)
            for i in range(NP):
                if i == 2:
                    pe.wait_ge(s_b2a, T)
                hidden_piece(3, 1, i)
            with pe.Fori(1, NX // 2 - 1) as pair:
                e = pair * 2
                output_layer(e, 0)
                hidden_layer(e + 2, 0)
                output_layer(e + 1, 1)
                hidden_layer(e + 3, 1)
            output_layer(NX - 2, 0)
            output_layer(NX - 1, 1)


_INS = ['x', 'src', 'dst', 'L0_gnn_W', 'L0_gnn_b', 'L0_ffn_Wr', 'L0_ffn_W1', 'L0_ffn_b1', 'L0_ffn_W2', 'L0_ffn_b2']


def kernel(**inputs):
    import concourse.bacc as _bacc
    from concourse.bass_utils import run_bass_kernel_spmd as _run

    nc = _bacc.Bacc("TRN2", target_bir_lowering=False, num_devices=1)
    arrays, args = {}, []
    for name in _INS:
        a = np.ascontiguousarray(inputs[name])
        arrays[f"in_{name}"] = a
        args.append(nc.dram_tensor(f"in_{name}", a.shape, mybir.dt.from_np(a.dtype), kind="ExternalInput").ap())
    args.append(nc.dram_tensor("out", inputs["x"].shape, F32, kind="ExternalOutput").ap())
    gnn_ffn(nc, *args)
    return _run(nc, [arrays], core_ids=[0]).results[0]["out"]
```
